# Optimizing a Trainium2 kernel written in Bass

```python
import numpy as np
import jax
import jax.numpy as jnp

def _softmax(x, axis=-1):
    return jax.nn.softmax(x, axis=axis)

def _gelu(x):
    return jax.nn.gelu(x, approximate=True)

def _silu(x):
    return jax.nn.silu(x)

def _sigmoid(x):
    return jax.nn.sigmoid(x)

def _layernorm(x, axis=-1, eps=1e-05):
    m = jnp.mean(x, axis=axis, keepdims=True)
    v = jnp.var(x, axis=axis, keepdims=True)
    return (x - m) / jnp.sqrt(v + eps)

def _scatter_add(tgt, idx, src, axis=0):
    return tgt.at[idx].add(src)

def _segment_sum(src, seg, n):
    return jax.ops.segment_sum(src, seg, n)
kernel_name = 'mk_flamingo_gated_d1_seqx_r8_6bb5d5'

def setup_inputs(seed: int=0):
    np.random.seed(seed)
    _w = jnp.asarray

    def _rec_inputs():
        import jax
        import jax.numpy as jnp
        _rk = jax.random.key(seed)
        x = -1.394e-06 + 0.9999 * jax.random.normal(jax.random.fold_in(_rk, 1), (64, 128, 128), jnp.float32)
        _lenS = 128 - jax.random.randint(jax.random.fold_in(_rk, 7), (64,), 0, max(1, 128 // 4) + 1, jnp.int32)
        _lenS2 = 77 - jax.random.randint(jax.random.fold_in(_rk, 8), (64,), 0, max(1, 77 // 4) + 1, jnp.int32)
        _ctx_1024P = jax.random.normal(jax.random.fold_in(_rk, 11), (64, 16, 128), jnp.float32)
        _ctx_1024c = jax.random.dirichlet(jax.random.fold_in(_rk, 511), 0.3 * jnp.ones((16,), jnp.float32), (64, 77))
        _ctx_1024t = jnp.einsum('bsk,bkd->bsd', _ctx_1024c, _ctx_1024P)
        _ctx_1024t = _ctx_1024t * jax.lax.rsqrt(jnp.mean(jnp.square(_ctx_1024t)) + 1e-12) * 0.953939
        ctx_1024 = -0.000292821 + 1.00034 * (_ctx_1024t + 0.3 * jax.random.normal(jax.random.fold_in(_rk, 611), (64, 77, 128), jnp.float32))
        _validS = jnp.arange(128)[None, :] < _lenS[:, None]
        _validS2 = jnp.arange(77)[None, :] < _lenS2[:, None]
        _causal = jnp.tril(jnp.ones((128, 128), dtype=bool))
        mask_1x1xSxS2_ik0 = jnp.where(jnp.broadcast_to(_validS2[0:1, None, None, :], (1, 1, 128, 77)), 0, 1).astype(jnp.int32)
        _g = jax.random.normal(jax.random.fold_in(_rk, 9001), (2, 1), jnp.float32)
        _g = jnp.sign(_g) * jnp.maximum(jnp.abs(_g), 1.0) + (_g == 0) * 1.0
        g_xattn = _g[0]
        g_ffn = _g[1]
        return (x, ctx_1024, mask_1x1xSxS2_ik0, g_xattn, g_ffn)
    x, ctx_1024, mask_1x1xSxS2_ik0, g_xattn, g_ffn = _rec_inputs()

    def _L0_xattn_setup():
        import jax, jax.numpy as jnp
        import numpy as np
        from math import sqrt
        HEADS = 16
        D_MODEL = 128
        HEAD_DIM = D_MODEL // HEADS
        B, SEQ = (2, 256)
        key = jax.random.key(seed)
        ks = jax.random.split(key, 8)
        k = jax.random.normal(ks[0], (B, SEQ, D_MODEL), dtype=jnp.float32)
        q = jax.random.normal(ks[1], (B, SEQ, D_MODEL), dtype=jnp.float32)
        v = jax.random.normal(ks[2], (B, SEQ, D_MODEL), dtype=jnp.float32)
        mask = jnp.tril(jnp.ones((SEQ, SEQ), dtype=jnp.int32))[None, None, :, :]
        s = 1.0 / sqrt(HEAD_DIM)
        Wq = jax.random.normal(ks[3], (HEAD_DIM, HEAD_DIM), dtype=jnp.float32) * s
        Wk = jax.random.normal(ks[4], (HEAD_DIM, HEAD_DIM), dtype=jnp.float32) * s
        Wv = jax.random.normal(ks[5], (HEAD_DIM, HEAD_DIM), dtype=jnp.float32) * s
        Wo = jax.random.normal(ks[6], (D_MODEL, D_MODEL), dtype=jnp.float32) * (1.0 / sqrt(D_MODEL))
        bo = jax.random.normal(ks[7], (D_MODEL,), dtype=jnp.float32) * 0.01
        return {'key': k, 'query': q, 'value': v, 'mask': mask, 'Wq': Wq, 'Wk': Wk, 'Wv': Wv, 'Wo': Wo, 'bo': bo}
    _L0_xattn_all = _L0_xattn_setup()
    _L0_xattn_in = {k: v for k, v in _L0_xattn_all.items() if k in ('Wq', 'Wk', 'Wv', 'Wo', 'bo')}
    del _L0_xattn_all

    def _L0_ffn_setup():
        import jax, jax.numpy as jnp
        import numpy as np
        D_MODEL = 128
        EXPERT_DIM = 256
        N_EXPERTS = 8
        LN_EPS = 1e-05

        def _bit_quant(W):
            scale = jnp.clip(jnp.mean(jnp.abs(W), axis=-1, keepdims=True), 1e-05, None)
            w_q = jnp.clip(jnp.round(W / scale), -1.0, 1.0) * scale
            return W + jax.lax.stop_gradient(w_q - W)
        key = jax.random.key(seed)
        ks = jax.random.split(key, 7)
        x = jax.random.normal(ks[0], (4, 256, D_MODEL), dtype=jnp.float32)
        shared_w1 = jax.random.normal(ks[1], (EXPERT_DIM, D_MODEL), dtype=jnp.float32) / np.sqrt(EXPERT_DIM)
        shared_w2 = jax.random.normal(ks[2], (D_MODEL, EXPERT_DIM), dtype=jnp.float32) / np.sqrt(D_MODEL)
        expert_w1 = jax.random.normal(ks[3], (N_EXPERTS, EXPERT_DIM, D_MODEL), dtype=jnp.float32) / np.sqrt(EXPERT_DIM)
        expert_w2 = jax.random.normal(ks[4], (N_EXPERTS, D_MODEL, EXPERT_DIM), dtype=jnp.float32) / np.sqrt(D_MODEL)
        router_w = 0.02 * jax.random.normal(ks[5], (N_EXPERTS, D_MODEL), dtype=jnp.float32)
        ln_gamma = jnp.ones((D_MODEL,), dtype=jnp.float32)
        ln_beta = jnp.zeros((D_MODEL,), dtype=jnp.float32)
        return {'x': x, 'shared_w1': shared_w1, 'shared_w2': shared_w2, 'expert_w1': expert_w1, 'expert_w2': expert_w2, 'router_w': router_w, 'ln_gamma': ln_gamma, 'ln_beta': ln_beta}
    _L0_ffn_all = _L0_ffn_setup()
    _L0_ffn_in = {k: v for k, v in _L0_ffn_all.items() if k in ('shared_w1', 'shared_w2', 'expert_w1', 'expert_w2', 'router_w', 'ln_gamma', 'ln_beta')}
    del _L0_ffn_all
    return {'x': x, 'ctx_1024': ctx_1024, 'mask_1x1xSxS2_ik0': mask_1x1xSxS2_ik0, 'g_xattn': g_xattn, 'g_ffn': g_ffn, 'L0_xattn_Wq': _L0_xattn_in['Wq'], 'L0_xattn_Wk': _L0_xattn_in['Wk'], 'L0_xattn_Wv': _L0_xattn_in['Wv'], 'L0_xattn_Wo': _L0_xattn_in['Wo'], 'L0_xattn_bo': _L0_xattn_in['bo'], 'L0_ffn_shared_w1': _L0_ffn_in['shared_w1'], 'L0_ffn_shared_w2': _L0_ffn_in['shared_w2'], 'L0_ffn_expert_w1': _L0_ffn_in['expert_w1'], 'L0_ffn_expert_w2': _L0_ffn_in['expert_w2'], 'L0_ffn_router_w': _L0_ffn_in['router_w'], 'L0_ffn_ln_gamma': _L0_ffn_in['ln_gamma'], 'L0_ffn_ln_beta': _L0_ffn_in['ln_beta']}

def reference(x, ctx_1024, mask_1x1xSxS2_ik0, g_xattn, g_ffn, L0_xattn_Wq, L0_xattn_Wk, L0_xattn_Wv, L0_xattn_Wo, L0_xattn_bo, L0_ffn_shared_w1, L0_ffn_shared_w2, L0_ffn_expert_w1, L0_ffn_expert_w2, L0_ffn_router_w, L0_ffn_ln_gamma, L0_ffn_ln_beta):
    import jax
    import jax.numpy as jnp

    def _L0_xattn_ref(key, query, value, mask, Wq, Wk, Wv, Wo, bo):
        import jax, jax.numpy as jnp
        import numpy as np
        from math import sqrt
        HEADS = 16
        D_MODEL = 128
        HEAD_DIM = D_MODEL // HEADS
        B, SEQ = (2, 256)
        b, q_len, d = query.shape
        k_len = key.shape[1]
        hd = d // HEADS
        k = key.reshape(b, k_len, HEADS, hd)
        q = query.reshape(b, q_len, HEADS, hd)
        v = value.reshape(b, k_len, HEADS, hd)
        k = jnp.einsum('bkhd,ed->bkhe', k, Wk)
        q = jnp.einsum('bqhd,ed->bqhe', q, Wq)
        v = jnp.einsum('bvhd,ed->bvhe', v, Wv)
        product = jnp.einsum('bqhd,bkhd->bhqk', q, k)
        product = jnp.where(mask == 0, jnp.float32(-1e+20), product)
        product = product / jnp.float32(sqrt(hd))
        score = jax.nn.softmax(product, axis=-1)
        out = jnp.einsum('bhqv,bvhd->bqhd', score, v).reshape(b, q_len, d)
        out = out @ Wo.T + bo
        return out

    def _L0_ffn_ref(x, shared_w1, shared_w2, expert_w1, expert_w2, router_w, ln_gamma, ln_beta):
        import jax, jax.numpy as jnp
        import numpy as np
        D_MODEL = 128
        EXPERT_DIM = 256
        N_EXPERTS = 8
        LN_EPS = 1e-05

        def _bit_quant(W):
            scale = jnp.clip(jnp.mean(jnp.abs(W), axis=-1, keepdims=True), 1e-05, None)
            w_q = jnp.clip(jnp.round(W / scale), -1.0, 1.0) * scale
            return W + jax.lax.stop_gradient(w_q - W)
        mu = jnp.mean(x, axis=-1, keepdims=True)
        var = jnp.mean(jnp.square(x - mu), axis=-1, keepdims=True)
        h = (x - mu) / jnp.sqrt(var + LN_EPS) * ln_gamma + ln_beta
        sw1, sw2 = (_bit_quant(shared_w1), _bit_quant(shared_w2))
        shared_out = jax.nn.silu(jnp.einsum('btd,fd->btf', h, sw1)) @ sw2.T
        probs = jax.nn.softmax(h @ router_w.T, axis=-1)
        top_prob = jnp.max(probs, axis=-1)
        top_idx = jnp.argmax(probs, axis=-1)
        ew1, ew2 = (_bit_quant(expert_w1), _bit_quant(expert_w2))
        h1 = jax.nn.silu(jnp.einsum('btd,efd->ebtf', h, ew1))
        eo = jnp.einsum('ebtf,edf->ebtd', h1, ew2)
        gate = jax.nn.one_hot(top_idx, N_EXPERTS, dtype=h.dtype) * top_prob[..., None]
        routed_out = jnp.einsum('ebtd,bte->btd', eo, gate)
        return shared_out + routed_out
    x = x + jnp.tanh(g_xattn[0]) * _L0_xattn_ref(ctx_1024, _layernorm(x, axis=-1), ctx_1024, mask_1x1xSxS2_ik0, L0_xattn_Wq, L0_xattn_Wk, L0_xattn_Wv, L0_xattn_Wo, L0_xattn_bo)
    x = x + jnp.tanh(g_ffn[0]) * _L0_ffn_ref(_layernorm(x, axis=-1), L0_ffn_shared_w1, L0_ffn_shared_w2, L0_ffn_expert_w1, L0_ffn_expert_w2, L0_ffn_router_w, L0_ffn_ln_gamma, L0_ffn_ln_beta)
    return x

_drawn_inputs = setup_inputs


def setup_inputs(seed=0):
    import zlib

    import numpy as np

    out = dict(_drawn_inputs(seed))
    spreads = {'L0_ffn_ln_gamma': (1.0, 0.2), 'L0_ffn_ln_beta': (0.0, 0.362)}
    factors = {'L0_xattn_bo': 7.789}
    for name, (base, spread) in spreads.items():
        noise = np.random.default_rng([zlib.crc32(name.encode()), seed]).standard_normal(out[name].shape)
        drawn = base * np.exp(spread * noise) if base else spread * noise
        out[name] = jnp.asarray(drawn.astype(out[name].dtype))
    for name, factor in factors.items():
        out[name] = (out[name] * factor).astype(out[name].dtype)
    return out
```

```python
import numpy as np
import concourse.bass as bass
from concourse import mybir
from contextlib import ExitStack

FP32 = mybir.dt.float32
BF16 = mybir.dt.bfloat16
I32 = mybir.dt.int32
ALU = mybir.AluOpType
ACT = mybir.ActivationFunctionType
AX = mybir.AxisListType

P = 128
B, SQ, D = 64, 128, 128
SK = 77
H = 16
HD = D // H
GH = 4
G = H // GH
GR = P // G
GK = GH * SK
QB = 4
NQ = B // QB
E, F = 8, 256
FB = F // P
NE = E + 1
EPS = 1e-5
MASKED = -1e20
BANK = 512


def ge(eng, sem, value):
    if not isinstance(value, int) or value > 0:
        eng.wait_ge(sem, value)


def build(nc, A):
    ctx = ExitStack()
    with ctx:
        def sb(name, shape, dt=FP32):
            return ctx.enter_context(nc.sbuf_tensor(name, shape, dt))

        def sem(name):
            return ctx.enter_context(nc.semaphore(name))

        PS = ctx.enter_context(nc.psum_tensor("PS", [P, 8, BANK], FP32))

        X = sb("X", [P, B, D])
        ctxq = sb("ctxq", [SK, 2, QB, D])
        HT = sb("HT", [P, B * P])
        ident = sb("ident", [P, P])
        identb = sb("identb", [P, P], BF16)
        ones = sb("ones", [P, BANK])
        headsel = sb("headsel", [P, H, HD])
        rowsel = sb("rowsel", [P, GH])
        shiftsel = sb("shiftsel", [P, GH])
        colsel = sb("colsel", [P, GH, GR])
        ind = sb("ind", [P, GH, SK])
        mask_i = sb("mask_i", [P, SK], I32)
        maskneg = sb("maskneg", [P, GH, SK], BF16)
        wq8 = sb("wq8", [P, HD])
        wk8 = sb("wk8", [P, HD])
        wv8 = sb("wv8", [P, HD])
        wq_bd = sb("wq_bd", [P, H, HD])
        wk_bd = sb("wk_bd", [P, H, HD])
        wv_bd = sb("wv_bd", [P, H, HD])
        wo_sb = sb("wo_sb", [P, D])
        woT = sb("woT", [P, D])
        MT = sb("MT", [P, P])
        WVO = sb("WVO", [P, D])
        gx = sb("gx", [P, 1])
        gf = sb("gf", [P, 1])
        tgx = sb("tgx", [P, 1])
        tgf = sb("tgf", [P, 1])
        bo = sb("bo", [P, D])
        gamma = sb("gamma", [P, 1])
        beta = sb("beta", [P, 1])
        w1n = sb("w1n", [P, NE, FB, D])
        w2n = sb("w2n", [P, NE, F])
        wabs = sb("wabs", [P, NE, FB])
        half = sb("half", [P, NE, FB])
        nhalf = sb("nhalf", [P, NE, FB])
        wabs2 = sb("wabs2", [P, NE])
        half2 = sb("half2", [P, NE])
        nhalf2 = sb("nhalf2", [P, NE])
        neg1 = sb("neg1", [P, NE, FB, D])
        W1T = sb("W1T", [P, NE, FB, P])
        W2T = sb("W2T", [P, NE, FB, P])
        rw = sb("rw", [E, D])
        hq = sb("hq", [P, BANK])
        carrier = sb("carrier", [P, 1])
        RWT = sb("RWT", [P, E])
        st = sb("st", [P, B, 6])
        mv = sb("mv", [P, B, 2])
        ve = sb("ve", [P, B])
        sd = sb("sd", [P, B])
        rstd = sb("rstd", [P, B])
        nmr = sb("nmr", [P, B])
        xn = sb("xn", [P, QB, D])
        xnT = sb("xnT", [P, 2, QB * P])
        ctxT = sb("ctxT", [P, QB * SK])
        kbd = sb("kbd", [P, 2, QB, GH, SK])
        vm = sb("vm", [SK, 2, G, GH, GR])
        nm = sb("nm", [P, 2, P])
        mT = sb("mT", [P, 2, P])
        prob = sb("prob", [P, 2, 2, GK])
        PT = sb("PT", [SK, 2, G, GH * P])
        rsum = sb("rsum", [P, P])
        oT = sb("oT", [P, P])
        lg = sb("lg", [P, B, E])
        lmax = sb("lmax", [P, B])
        eq = sb("eq", [P, B, E])
        rank = sb("rank", [P, E])
        best = sb("best", [P, B])
        gate = sb("gate", [P, B, E])
        topp = sb("topp", [P, B])
        h1 = sb("h1", [P, 2, FB, BANK])
        tmp = sb("tmp", [P, 2, QB, D])

        x_in, w_in, ffw_in = sem("x_in"), sem("w_in"), sem("ffw_in")
        ctx_in = [sem("ctx_in0"), sem("ctx_in1")]
        pool_c, dve_c = sem("pool_step"), sem("dve_step")
        consts_ready, var_ready, sd_ready, stats_ready = (sem(x) for x in ("consts_ready", "var_ready", "sd_ready", "stats_ready"))
        tanh_ready, bd_ready, wo_psum, wo_copied = (sem(x) for x in ("tanh_ready", "bd_ready", "wo_psum", "wo_copied"))
        wvo_psum, quantised, wT_psum, wT_copied = (sem(x) for x in ("wvo_psum", "quantised", "wT_psum", "wT_copied"))
        xb_ready, var2_ready, top_ready, gexp_ready, hT_kept = (sem(x) for x in ("xb_ready", "var2_ready", "top_ready", "gexp_ready", "hT_kept"))
        xn_ready, vm_ready = sem("xn_ready"), sem("vm_ready")
        prep_psum, prep_copied = sem("prep_psum"), sem("prep_copied")
        scores_ready, max_ready = sem("scores_ready"), sem("max_ready")
        mt_psum, mt_copied = sem("mt_psum"), sem("mt_copied")
        shifted, exp_done = sem("shifted"), sem("exp_done")
        pt_psum = [sem("pt_psum0"), sem("pt_psum1")]
        pt_copied = [sem("pt_copied0"), sem("pt_copied1")]
        pv_done, o_ready, proj_done, x1_done = sem("pv_done"), sem("o_ready"), sem("proj_done"), sem("x1_done")
        rs_done, x1_stats = sem("rs_done"), sem("x1_stats")
        h_ready, hT_psum, hT_copied, logits_done = sem("h_ready"), sem("hT_psum"), sem("hT_copied"), sem("logits_done")
        z_psum, silu_done, eo_psum, eo_read, acc_done = sem("z_psum"), sem("silu_done"), sem("eo_psum"), sem("eo_read"), sem("acc_done")
        out_done = sem("out_done")

        block = ctx.enter_context(nc.Block())
        N_W = 8 + 3 * H

        @block.sync
        def _(sp):
            for c in range(4):
                n = B // 4
                sp.dma_start(X[:, c * n:(c + 1) * n, :],
                             A["x"][c * n:(c + 1) * n].rearrange("b q d -> q b d")).then_inc(x_in, 16)

            def load_ctx(q, s):
                ge(sp, vm_ready, QB * (q - 1))
                ge(sp, prep_psum, 3 * (q - 2) + 2)
                sp.dma_start(ctxq[:, s], A["ctx"][bass.ds(q * QB, QB)].rearrange("b k d -> k b d")).then_inc(ctx_in[s], 16)

            load_ctx(0, 0)
            load_ctx(1, 1)
            with sp.Fori(0, (NQ - 2) // 2) as i2:
                load_ctx(2 * i2 + 2, 0)
                load_ctx(2 * i2 + 3, 1)
            with sp.Fori(0, NQ) as qi:
                sp.wait_ge(acc_done, (qi + 1) * E)
                sp.dma_start(A["out"][bass.ds(qi * QB, QB)].rearrange("b q d -> q b d"),
                             X[:, bass.ds(qi * QB, QB), :]).then_inc(out_done, 16)
            sp.wait_ge(out_done, 16 * NQ)

        @block.gpsimd
        def _(pool):
            n = [0]

            def step(ins):
                n[0] += 1
                ins.then_inc(pool_c, 1)
                pool.wait_ge(pool_c, n[0])

            def band(t, pattern, base_lo, base_hi, cm):
                step(nc.gpsimd.affine_select(out=t, in_=t, compare_op=ALU.is_ge, fill=0.0, base=base_lo,
                                             pattern=pattern, channel_multiplier=cm))
                step(nc.gpsimd.affine_select(out=t, in_=t, compare_op=ALU.is_ge, fill=0.0, base=base_hi,
                                             pattern=[[-s, c] for s, c in pattern], channel_multiplier=-cm))

            step(nc.gpsimd.memset(ident[:], 0.0))
            step(nc.gpsimd.affine_select(out=ident[:], in_=ident[:], compare_op=ALU.not_equal, fill=1.0,
                                         base=0, pattern=[[-1, P]], channel_multiplier=1))
            step(nc.gpsimd.memset(headsel[:], 1.0))
            band(headsel[:], [[-HD, H], [0, HD]], 0, HD - 1, 1)
            step(nc.gpsimd.memset(colsel[:], 1.0))
            band(colsel[:], [[-HD, GH], [1, GR]], 0, HD - 1, 0)
            step(nc.gpsimd.memset(nm[:], 0.0))
            for i in range(E):
                step(nc.gpsimd.memset(rank[:, i:i + 1], float(E - i)))
            step(nc.gpsimd.tensor_tensor(rowsel[:], headsel[:, 0:GH, 0], headsel[:, GH:2 * GH, 0], ALU.add))
            for g in range(2, G):
                step(nc.gpsimd.tensor_tensor(rowsel[:], rowsel[:], headsel[:, g * GH:(g + 1) * GH, 0], ALU.add))
            step(nc.gpsimd.tensor_tensor(shiftsel[:], ident[:, 0:GH], ident[:, GR:GR + GH], ALU.add))
            for g in range(2, G):
                step(nc.gpsimd.tensor_tensor(shiftsel[:], shiftsel[:], ident[:, g * GR:g * GR + GH], ALU.add))
            step(nc.gpsimd.tensor_copy(ind[:], shiftsel[:].unsqueeze(2).broadcast_to([P, GH, SK])))
            step(nc.gpsimd.tensor_copy(identb[:], ident[:]))
            pool.sem_inc(consts_ready, 1)

            pool.wait_ge(bd_ready, 1)

            def make_vm(b, j, s):
                ge(pool, pv_done, b - 1)
                v = ctxq[:, s, j, :].rearrange("k (g c) -> k g c", g=G)
                nc.gpsimd.tensor_tensor(vm[:, j % 2], v.unsqueeze(2).broadcast_to([SK, G, GH, GR]),
                                        colsel[0:SK].unsqueeze(1).broadcast_to([SK, G, GH, GR]),
                                        ALU.mult).then_inc(vm_ready, 1)
                xb = X[:, bass.ds(b, 1), :].squeeze(1)
                nc.gpsimd.tensor_tensor(xb, xb, bo[:], ALU.add).then_inc(xb_ready, 1)

            def quad(q, s, arrived, last=False):
                pool.wait_ge(xn_ready, q + 1)
                pool.wait_ge(ctx_in[s], 16 * arrived)
                for j in range(QB):
                    make_vm(q * QB + j, j, s)

            quad(0, 0, 1)
            with pool.Fori(0, (NQ - 2) // 2) as i2:
                quad(2 * i2 + 1, 1, i2 + 1)
                quad(2 * i2 + 2, 0, i2 + 2)
            quad(NQ - 1, 1, NQ // 2, last=True)

            def acc(q, e):
                pool.wait_ge(eo_read, q * NE + e + 2)
                if e >= 1:
                    pool.wait_ge(acc_done, q * E + e)
                nc.gpsimd.tensor_tensor(carrier[:], rank[:, 0:1], rank[:, 0:1], ALU.add)
                nc.gpsimd.tensor_tensor(X[:, bass.ds(q * QB, QB), :], X[:, bass.ds(q * QB, QB), :],
                                        tmp[:, e % 2], ALU.add).then_inc(acc_done, 1)
            with pool.Fori(0, NQ) as qi:
                for e in range(E):
                    acc(qi, e)

        @block.vector
        def _(dve):
            n = [0]

            def step(ins, signal=None):
                if signal is not None:
                    ins.then_inc(signal, 1)
                    dve.wait_ge(signal, 1)
                    return
                n[0] += 1
                ins.then_inc(dve_c, 1)
                dve.wait_ge(dve_c, n[0])

            def newton(v, inv):
                step(nc.vector.tensor_tensor(sd[:], inv, inv, ALU.mult))
                step(nc.vector.tensor_tensor(sd[:], sd[:], v, ALU.mult))
                step(nc.vector.tensor_scalar(sd[:], sd[:], -0.5, 1.5, ALU.mult, ALU.add))
                step(nc.vector.tensor_tensor(inv, inv, sd[:], ALU.mult))

            dve.wait_ge(x_in, 64)
            for b in range(B):
                ins = nc.vector.bn_stats(st[:, b, :], X[:, b, :])
            step(ins)
            for b in range(B):
                ins = nc.vector.bn_aggr(mv[:, b, :], st[:, b, :])
            step(ins)
            step(nc.vector.tensor_scalar(ve[:], mv[:, :, 1], EPS, None, ALU.add), var_ready)
            dve.wait_ge(sd_ready, 1)
            step(nc.vector.reciprocal(rstd[:], sd[:]))
            newton(ve[:], rstd[:])
            step(nc.vector.scalar_tensor_tensor(nmr[:], mv[:, :, 0], -1.0, rstd[:], ALU.mult, ALU.mult), stats_ready)

            dve.wait_ge(w_in, 16 * N_W)
            dve.wait_ge(consts_ready, 1)
            for bd, w in ((wq_bd, wq8), (wk_bd, wk8), (wv_bd, wv8)):
                ins = nc.vector.tensor_tensor(bd[:], w[:].unsqueeze(1).broadcast_to([P, H, HD]), headsel[:], ALU.mult)
            step(ins)
            step(nc.vector.tensor_scalar(maskneg[:], mask_i[:].unsqueeze(1).broadcast_to([P, GH, SK]), 0.0, MASKED,
                                         ALU.is_equal, ALU.mult))
            dve.wait_ge(tanh_ready, 1)
            step(nc.vector.tensor_scalar(bo[:], bo[:], tgx[:], None, ALU.mult), bd_ready)
            dve.wait_ge(wo_psum, 1)
            step(nc.vector.tensor_copy(woT[:], PS[:, 0, 0:P]))
            step(nc.vector.tensor_copy(MT[:], PS[:, 1, 0:P]), wo_copied)
            dve.wait_ge(wvo_psum, 1)
            step(nc.vector.tensor_scalar(WVO[:], PS[:, 0, 0:D], tgx[:], None, ALU.mult))

            dve.wait_ge(ffw_in, 16 * 4)
            step(nc.vector.tensor_reduce(wabs[:], w1n[:], AX.X, ALU.add, apply_absolute_value=True))
            step(nc.vector.tensor_reduce(wabs2[:], w2n[:], AX.X, ALU.add, apply_absolute_value=True))
            step(nc.vector.tensor_scalar(wabs[:], wabs[:], 1.0 / D, 1e-5, ALU.mult, ALU.max))
            step(nc.vector.tensor_scalar(wabs2[:], wabs2[:], 1.0 / F, 1e-5, ALU.mult, ALU.max))
            for s, hh, nh in ((wabs, half, nhalf), (wabs2, half2, nhalf2)):
                step(nc.vector.tensor_scalar(hh[:], s[:], 0.5, None, ALU.mult))
                step(nc.vector.tensor_scalar(nh[:], s[:], -0.5, None, ALU.mult))
            step(nc.vector.tensor_scalar(wabs2[:], wabs2[:], tgf[:], None, ALU.mult))

            def quantise(w, s, hh, nh, neg, signal=None):
                shape = list(w.shape)
                step(nc.vector.tensor_tensor(neg, w, nh.broadcast_to(shape), ALU.is_lt))
                step(nc.vector.tensor_tensor(w, w, hh.broadcast_to(shape), ALU.is_gt))
                step(nc.vector.tensor_tensor(w, w, neg, ALU.subtract))
                step(nc.vector.tensor_tensor(w, w, s.broadcast_to(shape), ALU.mult), signal)

            quantise(w1n[:], wabs[:].unsqueeze(3), half[:].unsqueeze(3), nhalf[:].unsqueeze(3), neg1[:])
            quantise(w2n[:], wabs2[:].unsqueeze(2), half2[:].unsqueeze(2), nhalf2[:].unsqueeze(2),
                     neg1[:].rearrange("p e b d -> p e (b d)"), quantised)
            for e in range(NE):
                dve.wait_ge(wT_psum, e + 1)
                nc.vector.tensor_copy(W1T[:, e], PS[:, 2 * (e % 2), 0:F])
                nc.vector.tensor_copy(W2T[:, e], PS[:, 2 * (e % 2) + 1, 0:F]).then_inc(wT_copied, 1)
            dve.wait_ge(wT_psum, NE + 1)
            nc.vector.tensor_copy(RWT[:], PS[:, 4, 0:E]).then_inc(wT_copied, 1)

            def make_xn(q):
                ge(dve, prep_psum, 3 * (q - 1) + 1)
                for j in range(QB):
                    b = q * QB + j
                    ins = nc.vector.tensor_scalar(xn[:, j, :], X[:, bass.ds(b, 1), :].squeeze(1),
                                                  rstd[:, bass.ds(b, 1)], nmr[:, bass.ds(b, 1)], ALU.mult, ALU.add)
                ins.then_inc(xn_ready, 1)

            def prep_x(q, qs):
                dve.wait_ge(prep_psum, 3 * q + 1)
                nc.vector.tensor_copy(xnT[:, qs], PS[:, 6, :]).then_inc(prep_copied, 1)

            def prep_ctx(q):
                dve.wait_ge(prep_psum, 3 * q + 2)
                nc.vector.tensor_copy(ctxT[:], PS[:, 6, 0:QB * SK]).then_inc(prep_copied, 1)

            def prep_k(q, qs):
                dve.wait_ge(prep_psum, 3 * q + 3)
                kp = PS[:, 6, 0:QB * SK].rearrange("p (b k) -> p b k", b=QB)
                nc.vector.tensor_tensor(kbd[:, qs], kp.unsqueeze(2).broadcast_to([P, QB, GH, SK]),
                                        rowsel[:].unsqueeze(1).unsqueeze(3).broadcast_to([P, QB, GH, SK]),
                                        ALU.mult).then_inc(prep_copied, 1)

            def take_max(b, u):
                dve.wait_ge(scores_ready, 2 * b + u + 1)
                ge(dve, mt_psum, 2 * (b - 1) + u + 1)
                nc.vector.tensor_reduce(
                    nm[:, u, :].rearrange("p (g r) -> p g r", g=G)[:, 2 * u:2 * u + 2, 0:GH],
                    PS[:, 2 * u:2 * u + 2, 0:GK].rearrange("p g (i k) -> p g i k", k=SK),
                    AX.X, ALU.max, negate=True).then_inc(max_ready, 1)

            def copy_pt(b, s, u):
                dve.wait_ge(pt_psum[1], 2 * b + u + 1)
                ge(dve, pv_done, b - 1)
                nc.vector.tensor_copy(PT[:, s, 2 * u + 1, :], PS[0:SK, 5, :]).then_inc(pt_copied[1], 1)

            def finish(b):
                dve.wait_ge(pv_done, b + 1)
                nc.vector.reciprocal(rsum[:], PS[:, 7, P:2 * P]).then_inc(rs_done, 1)
                dve.wait_ge(rs_done, b + 1)
                nc.vector.tensor_tensor(oT[:], PS[:, 7, 0:P], rsum[:], ALU.mult).then_inc(o_ready, 1)

            def residual(b):
                dve.wait_ge(proj_done, b + 1)
                dve.wait_ge(xb_ready, b + 1)
                xb = X[:, bass.ds(b, 1), :].squeeze(1)
                nc.vector.tensor_tensor(xb, xb, PS[:, 7, 2 * P:3 * P], ALU.add).then_inc(x1_done, 1)
                dve.wait_ge(x1_done, b + 1)
                nc.vector.bn_stats(st[:, bass.ds(b, 1), :].squeeze(1), xb).then_inc(x1_stats, 1)

            make_xn(0)
            prep_x(0, 0)
            prep_ctx(0)
            prep_k(0, 0)

            def quad(q, q2, last=False):
                for j in range(QB):
                    b = q * QB + j
                    first = isinstance(b, int) and b == 0
                    if j == 0 and not last:
                        make_xn(q + 1)
                    take_max(b, 0)
                    if not first:
                        copy_pt(b - 1, (j - 1) % 2, 0)
                    take_max(b, 1)
                    if not first:
                        copy_pt(b - 1, (j - 1) % 2, 1)
                    if not last:
                        if j == 0:
                            prep_x(q + 1, 1 - q2)
                        if j == 1:
                            prep_ctx(q + 1)
                        if j == 2:
                            prep_k(q + 1, 1 - q2)
                    if not first:
                        finish(b - 1)
                        residual(b - 1)

            quad(0, 0)
            with dve.Fori(0, (NQ - 2) // 2) as i2:
                quad(2 * i2 + 1, 1)
                quad(2 * i2 + 2, 0)
            quad(NQ - 1, 1, last=True)
            for u in range(2):
                copy_pt(B - 1, 1, u)
            finish(B - 1)
            residual(B - 1)

            dve.wait_ge(x1_stats, B)
            for b in range(B):
                ins = nc.vector.bn_aggr(mv[:, b, :], st[:, b, :])
            step(ins)
            step(nc.vector.tensor_scalar(ve[:], mv[:, :, 1], 1.0 + EPS, EPS * EPS, ALU.mult, ALU.add), var2_ready)
            dve.wait_ge(sd_ready, 2)
            step(nc.vector.reciprocal(rstd[:], sd[:]))
            newton(ve[:], rstd[:])
            step(nc.vector.scalar_tensor_tensor(nmr[:], mv[:, :, 0], -1.0, rstd[:], ALU.mult, ALU.mult))
            with dve.Fori(0, NQ) as qi:
                dve.wait_ge(hT_psum, qi)
                for j in range(QB):
                    b = qi * QB + j
                    ins = nc.vector.tensor_scalar(xn[:, j, :], X[:, bass.ds(b, 1), :].squeeze(1),
                                                  rstd[:, bass.ds(b, 1)], nmr[:, bass.ds(b, 1)], ALU.mult, ALU.add)
                ins.then_inc(h_ready, 1)
                dve.wait_ge(hT_copied, qi + 1)
                nc.vector.tensor_copy(HT[:, bass.ds(qi * BANK, BANK)], hq[:]).then_inc(hT_kept, 1)
            dve.wait_ge(logits_done, NQ)
            lgp = PS[:, 4, :].rearrange("p (b e) -> p b e", e=E)
            step(nc.vector.tensor_reduce(lmax[:], lgp, AX.X, ALU.max))
            step(nc.vector.tensor_tensor(lg[:], lgp, lmax[:].unsqueeze(2).broadcast_to([P, B, E]), ALU.subtract))
            step(nc.vector.tensor_scalar(eq[:], lg[:], 0.0, None, ALU.is_equal))
            step(nc.vector.tensor_tensor(eq[:], eq[:], rank[:].unsqueeze(1).broadcast_to([P, B, E]), ALU.mult))
            step(nc.vector.tensor_reduce(best[:], eq[:], AX.X, ALU.max))
            step(nc.vector.tensor_tensor(eq[:], eq[:], best[:].unsqueeze(2).broadcast_to([P, B, E]), ALU.is_equal), top_ready)
            dve.wait_ge(gexp_ready, 1)
            step(nc.vector.tensor_reduce(topp[:], gate[:], AX.X, ALU.add))
            step(nc.vector.reciprocal(topp[:], topp[:]))
            step(nc.vector.tensor_tensor(gate[:], eq[:], topp[:].unsqueeze(2).broadcast_to([P, B, E]), ALU.mult))

            with dve.Fori(0, NQ) as qi:
                xq = X[:, bass.ds(qi * QB, QB), :]
                for k in range(NE):
                    dve.wait_ge(eo_psum, qi * NE + k + 1)
                    eo = PS[:, 2 + k % 2, :].rearrange("p (b d) -> p b d", b=QB)
                    if k == 0:
                        nc.vector.tensor_tensor(xq, xq, eo, ALU.add).then_inc(eo_read, 1)
                    else:
                        e = k - 1
                        dve.wait_ge(acc_done, qi * E + e - 1 if e >= 2 else qi * E)
                        nc.vector.tensor_tensor(tmp[:, e % 2], eo,
                                                gate[:, bass.ds(qi * QB, QB), e:e + 1].broadcast_to([P, QB, D]),
                                                ALU.mult).then_inc(eo_read, 1)

        @block.scalar
        def _(act):
            act.dma_start(wo_sb[:], A["Wo"][:, :]).then_inc(w_in, 16)
            act.dma_start(mask_i[:], A["mask"][0, 0]).then_inc(w_in, 16)
            for t, name in ((wq8, "Wq"), (wk8, "Wk"), (wv8, "Wv")):
                for hh in range(H):
                    act.dma_start(t[hh * HD:(hh + 1) * HD, :], A[name][:, :]).then_inc(w_in, 16)
            act.dma_start(gx[:], A["g_x"].unsqueeze(0).broadcast_to([P, 1])).then_inc(w_in, 16)
            act.dma_start(gf[:], A["g_f"].unsqueeze(0).broadcast_to([P, 1])).then_inc(w_in, 16)
            act.dma_start(bo[:], A["bo"].unsqueeze(0).broadcast_to([P, D])).then_inc(w_in, 16)
            act.dma_start(gamma[:], A["gamma"].unsqueeze(1)).then_inc(w_in, 16)
            act.dma_start(beta[:], A["beta"].unsqueeze(1)).then_inc(w_in, 16)
            act.dma_start(rw[:], A["rw"][:, :]).then_inc(w_in, 16)
            act.dma_start(w1n[:, 0:E], A["ew1"].rearrange("e (b p) d -> p e b d", p=P)).then_inc(ffw_in, 16)
            act.dma_start(w1n[:, E], A["sw1"].rearrange("(b p) d -> p b d", p=P)).then_inc(ffw_in, 16)
            act.dma_start(w2n[:, 0:E], A["ew2"].rearrange("e d f -> d e f")).then_inc(ffw_in, 16)
            act.dma_start(w2n[:, E], A["sw2"][:, :]).then_inc(ffw_in, 16)

            act.wait_ge(var_ready, 1)
            nc.scalar.activation(sd[:], ve[:], ACT.Sqrt).then_inc(sd_ready, 1)
            act.wait_ge(w_in, 16 * N_W)
            nc.scalar.activation(tgx[:], gx[:], ACT.Tanh)
            nc.scalar.activation(tgf[:], gf[:], ACT.Tanh).then_inc(tanh_ready, 1)

            def copy_pt(b, s, u):
                act.wait_ge(pt_psum[0], 2 * b + u + 1)
                ge(act, pv_done, b - 1)
                nc.scalar.copy(PT[:, s, 2 * u, :], PS[0:SK, 4, :]).then_inc(pt_copied[0], 1)

            def copy_mt(b, u):
                act.wait_ge(mt_psum, 2 * b + u + 1)
                ge(act, shifted, 2 * (b - 1) + u + 1)
                nc.scalar.copy(mT[:, u, :], PS[:, 6, 0:P]).then_inc(mt_copied, 1)

            def exps(b, u):
                act.wait_ge(shifted, 2 * b + u + 1)
                for v in range(2):
                    ge(act, pt_psum[v], 2 * (b - 1) + u + 1)
                nc.scalar.activation(prob[:, u], PS[:, 2 * u:2 * u + 2, 0:GK], ACT.Exp,
                                     scale=float(1.0 / np.sqrt(HD))).then_inc(exp_done, 1)

            def quad(q):
                for j in range(QB):
                    b = q * QB + j
                    first = isinstance(b, int) and b == 0
                    for u in range(2):
                        if not first:
                            copy_pt(b - 1, (j - 1) % 2, u)
                        copy_mt(b, u)
                        exps(b, u)

            quad(0)
            with act.Fori(1, NQ) as qi:
                quad(qi)
            for u in range(2):
                copy_pt(B - 1, 1, u)

            act.wait_ge(var2_ready, 1)
            nc.scalar.activation(sd[:], ve[:], ACT.Sqrt).then_inc(sd_ready, 1)
            with act.Fori(0, NQ) as qi:
                act.wait_ge(hT_psum, qi + 1)
                act.wait_ge(logits_done, qi)
                act.wait_ge(hT_kept, qi)
                nc.scalar.activation(hq[:], PS[:, 5, :], ACT.Identity,
                                     bias=beta[:], scale=gamma[:]).then_inc(hT_copied, 1)
            act.wait_ge(top_ready, 1)
            nc.scalar.activation(gate[:], lg[:], ACT.Exp).then_inc(gexp_ready, 1)

            with act.Fori(0, NQ) as qi:
                for k in range(NE):
                    for f in range(FB):
                        act.wait_ge(z_psum, (qi * NE + k) * FB + f + 1)
                        if f == 0 and k >= 2:
                            act.wait_ge(eo_psum, qi * NE + k - 1)
                        elif f == 0:
                            act.wait_ge(eo_psum, qi * NE)
                        nc.scalar.activation(h1[:, k % 2, f, :], PS[:, 6 * f + k % 2, :],
                                             ACT.Silu).then_inc(silu_done, 1)

        @block.tensor
        def _(pe):
            pe.wait_ge(bd_ready, 1)
            nc.tensor.transpose(PS[:, 0, 0:P], wo_sb[:], ident[:])
            nc.tensor.matmul(PS[:, 1, 0:P], wk_bd[:].rearrange("p h d -> p (h d)"),
                             wq_bd[:].rearrange("p h d -> p (h d)"), start=True, stop=True).then_inc(wo_psum, 1)
            pe.wait_ge(wo_copied, 1)
            nc.tensor.matmul(PS[:, 0, 0:P], wv_bd[:].rearrange("p h d -> p (h d)"), woT[:],
                             start=True, stop=True).then_inc(wvo_psum, 1)
            pe.wait_ge(quantised, 1)
            for e in range(NE):
                if e >= 2:
                    pe.wait_ge(wT_copied, e - 1)
                for f in range(FB):
                    nc.tensor.transpose(PS[:, 2 * (e % 2), f * P:(f + 1) * P], w1n[:, e, f, :], ident[:])
                for f in range(FB):
                    ins = nc.tensor.transpose(PS[:, 2 * (e % 2) + 1, f * P:(f + 1) * P],
                                              w2n[:, e, f * P:(f + 1) * P], ident[:])
                ins.then_inc(wT_psum, 1)
            nc.tensor.transpose(PS[:, 4, 0:E], rw[:], ident[0:E, 0:E]).then_inc(wT_psum, 1)

            pe.wait_ge(wT_copied, NE + 1)

            def prep(q, qs, part, arrived):
                ge(pe, prep_copied, 3 * q + part)
                if part == 0:
                    pe.wait_ge(xn_ready, q + 1)
                    for j in range(QB):
                        ins = nc.tensor.transpose(PS[:, 6, j * P:(j + 1) * P], xn[:, j, :], ident[:])
                elif part == 1:
                    pe.wait_ge(ctx_in[qs], 16 * arrived)
                    for j in range(QB):
                        ins = nc.tensor.transpose(PS[:, 6, j * SK:(j + 1) * SK],
                                                  ctxq[:, qs, j, :], ident[0:SK, 0:SK])
                else:
                    ins = nc.tensor.matmul(PS[:, 6, 0:QB * SK], MT[:], ctxT[:], start=True, stop=True)
                ins.then_inc(prep_psum, 1)

            def scores(b, j, qs, u):
                ge(pe, exp_done, 2 * (b - 1) + u + 1)
                for g in (2 * u, 2 * u + 1):
                    nc.tensor.matmul(PS[:, g, 0:GK], identb[:], maskneg[:].rearrange("p i k -> p (i k)"),
                                     start=True, stop=False)
                for g in (2 * u, 2 * u + 1):
                    r = slice(g * GR, (g + 1) * GR)
                    ins = nc.tensor.matmul(PS[:, g, 0:GK], xnT[r, qs, j * P:(j + 1) * P],
                                           kbd[r, qs, j].rearrange("p i k -> p (i k)"), start=False, stop=True,
                                           tile_position=(g * GR, 0))
                ins.then_inc(scores_ready, 1)

            def shift(b, u, prepared):
                pe.wait_ge(max_ready, 2 * b + u + 1)
                ge(pe, prep_copied, prepared)
                ge(pe, mt_copied, 2 * b + u)
                nc.tensor.transpose(PS[:, 6, 0:P], nm[:, u, :], ident[:]).then_inc(mt_psum, 1)
                pe.wait_ge(mt_copied, 2 * b + u + 1)
                for g in (2 * u, 2 * u + 1):
                    r = slice(g * GR, (g + 1) * GR)
                    ins = nc.tensor.matmul(PS[:, g, 0:GK], mT[r, u, :], ind[r].rearrange("p i k -> p (i k)"),
                                           start=False, stop=True, tile_position=(g * GR, 0),
                                           skip_group_check=True)
                ins.then_inc(shifted, 1)

            def transpose_probs(b, u):
                pe.wait_ge(exp_done, 2 * b + u + 1)
                for v in range(2):
                    ge(pe, pt_copied[v], 2 * b + u)
                    for i in range(GH):
                        ins = nc.tensor.transpose(PS[0:SK, 4 + v, i * P:(i + 1) * P],
                                                  prob[:, u, v, i * SK:(i + 1) * SK], ident[:])
                    ins.then_inc(pt_psum[v], 1)

            def weigh(b, s):
                for v in range(2):
                    pe.wait_ge(pt_copied[v], 2 * b + 2)
                pe.wait_ge(vm_ready, b + 1)
                ge(pe, x1_done, b)
                for what in range(2):
                    for i in range(GH):
                        for g in range(G):
                            ins = nc.tensor.matmul(
                                PS[g * GR:(g + 1) * GR, 7, what * P:(what + 1) * P],
                                vm[:, s, g, i, :] if what == 0 else colsel[0:SK, i, :],
                                PT[:, s, g, i * P:(i + 1) * P], start=i == 0, stop=i == GH - 1,
                                tile_position=(0, g * GR))
                ins.then_inc(pv_done, 1)

            def project(b):
                pe.wait_ge(o_ready, b + 1)
                nc.tensor.matmul(PS[:, 7, 2 * P:2 * P + D], oT[:], WVO[:], start=True, stop=True).then_inc(proj_done, 1)

            for part in range(3):
                prep(0, 0, part, 1)

            def quad(q, q2, arrived=None, last=False):
                for j in range(QB):
                    b = q * QB + j
                    first = isinstance(b, int) and b == 0
                    s = (j - 1) % 2
                    if j == 0:
                        pe.wait_ge(prep_copied, 3 * q + 3)
                    scores(b, j, q2, 0)
                    if not first:
                        transpose_probs(b - 1, 0)
                    scores(b, j, q2, 1)
                    shift(b, 0, 3 * (q + 1) + min(j, 3) if not last else 3 * (q + 1))
                    if not first:
                        transpose_probs(b - 1, 1)
                    shift(b, 1, 0)
                    if not first:
                        weigh(b - 1, s)
                    if not last and j < 3:
                        pe.wait_ge(mt_copied, 2 * b + 2)
                        prep(q + 1, 1 - q2, j, arrived)
                    if not first:
                        project(b - 1)

            quad(0, 0, 1)
            with pe.Fori(0, (NQ - 2) // 2) as i2:
                quad(2 * i2 + 1, 1, i2 + 2)
                quad(2 * i2 + 2, 0, i2 + 2)
            quad(NQ - 1, 1, last=True)
            for u in range(2):
                transpose_probs(B - 1, u)
            weigh(B - 1, 1)
            project(B - 1)

            pe.wait_ge(pt_copied[1], 2 * B)
            with pe.Fori(0, NQ) as qi:
                pe.wait_ge(h_ready, qi + 1)
                pe.wait_ge(hT_copied, qi)
                for j in range(QB):
                    ins = nc.tensor.transpose(PS[:, 5, j * P:(j + 1) * P], xn[:, j, :], ident[:])
                ins.then_inc(hT_psum, 1)
                pe.wait_ge(hT_copied, qi + 1)
                for j in range(QB):
                    ins = nc.tensor.matmul(PS[:, 4, bass.ds(qi * QB * E + j * E, E)],
                                           hq[:, j * P:(j + 1) * P], RWT[:], start=True, stop=True)
                ins.then_inc(logits_done, 1)

            with pe.Fori(0, NQ) as qi:
                for k in range(NE):
                    e = E if k == 0 else k - 1
                    for f in range(FB):
                        if k >= 2:
                            pe.wait_ge(silu_done, (qi * NE + k - 2) * FB + f + 1)
                        else:
                            pe.wait_ge(silu_done, qi * NE * FB)
                        nc.tensor.matmul(PS[:, k % 2 + 6 * f, :], W1T[:, e, f, :], HT[:, bass.ds(qi * BANK, BANK)],
                                         start=True, stop=True).then_inc(z_psum, 1)
                    if k >= 2:
                        pe.wait_ge(eo_read, qi * NE + k - 1)
                    else:
                        pe.wait_ge(eo_read, qi * NE)
                    pe.wait_ge(silu_done, (qi * NE + k) * FB + FB)
                    for j in range(QB):
                        for f in range(FB):
                            ins = nc.tensor.matmul(PS[:, 2 + k % 2, j * P:(j + 1) * P], h1[:, k % 2, f, j * P:(j + 1) * P],
                                                   W2T[:, e, f, :], start=f == 0, stop=f == FB - 1)
                    ins.then_inc(eo_psum, 1)


NAMES = {"x": "x", "ctx": "ctx_1024", "mask": "mask_1x1xSxS2_ik0", "g_x": "g_xattn", "g_f": "g_ffn",
         "Wq": "L0_xattn_Wq", "Wk": "L0_xattn_Wk", "Wv": "L0_xattn_Wv", "Wo": "L0_xattn_Wo", "bo": "L0_xattn_bo",
         "sw1": "L0_ffn_shared_w1", "sw2": "L0_ffn_shared_w2", "ew1": "L0_ffn_expert_w1",
         "ew2": "L0_ffn_expert_w2", "rw": "L0_ffn_router_w", "gamma": "L0_ffn_ln_gamma", "beta": "L0_ffn_ln_beta"}


def kernel(**inputs):
    import concourse.bacc as bacc
    from concourse.bass_utils import run_bass_kernel_spmd

    nc = bacc.Bacc("TRN2", target_bir_lowering=False, num_devices=1)
    arrays, args = {}, {}
    for short, name in NAMES.items():
        a = np.ascontiguousarray(inputs[name])
        arrays[f"in_{short}"] = a
        args[short] = nc.dram_tensor(f"in_{short}", a.shape, mybir.dt.from_np(a.dtype), kind="ExternalInput").ap()
    args["out"] = nc.dram_tensor("out", (B, SQ, D), FP32, kind="ExternalOutput").ap()
    build(nc, args)
    r = run_bass_kernel_spmd(nc, [arrays], core_ids=[0])
    return r.results[0]["out"]
```

```python
import numpy as np
import concourse.bass as bass
from concourse import mybir
from contextlib import ExitStack

FP32 = mybir.dt.float32
BF16 = mybir.dt.bfloat16
I32 = mybir.dt.int32
FP32R = mybir.dt.float32r
ALU = mybir.AluOpType
ACT = mybir.ActivationFunctionType
AX = mybir.AxisListType

P = 128
B, SQ, D = 64, 128, 128
SK = 77
H = 16
HD = D // H
GH = 4
G = H // GH
GR = P // G
GK = GH * SK
SP = SK + 1
RN = SP // 6
QB = 4
NQ = B // QB
XC = 8
E, F = 8, 256
FB = F // P
NE = E + 1
EPS = 1e-5
TOKENS = B * SQ
REGION = TOKENS + P
ROW = D + 4
NT = -(-(TOKENS // P + E - 1) // 12) * 12
PAYS = 4
SLOTS = 6
NG = NT // 2 // SLOTS
MASKED = -1e20
BANK = 512


def ge(eng, sem, value):
    if not isinstance(value, int) or value > 0:
        eng.wait_ge(sem, value)


def build(nc, A):
    ctx = ExitStack()
    with ctx:
        def sb(name, shape, dt=FP32):
            return ctx.enter_context(nc.sbuf_tensor(name, shape, dt))

        def sem(name):
            return ctx.enter_context(nc.semaphore(name))

        PS = ctx.enter_context(nc.psum_tensor("PS", [P, 8, BANK], FP32))

        X = sb("X", [P, B, D])
        ctxq = sb("ctxq", [SK, 2, QB, D])
        ident = sb("ident", [P, P])
        identb = sb("identb", [P, P], BF16)
        ones = sb("ones", [P, P])
        headsel = sb("headsel", [P, H, HD])
        rowsel = sb("rowsel", [P, GH])
        shiftsel = sb("shiftsel", [P, GH])
        ind = sb("ind", [P, GH, SK], FP32R)
        mask_i = sb("mask_i", [P, SK], I32)
        maskneg = sb("maskneg", [P, GH, SK], BF16)
        wq8 = sb("wq8", [P, HD])
        wk8 = sb("wk8", [P, HD])
        wv8 = sb("wv8", [P, HD])
        wq_bd = sb("wq_bd", [P, H, HD])
        wk_bd = sb("wk_bd", [P, H, HD])
        wv_bd = sb("wv_bd", [P, H, HD])
        wo_sb = sb("wo_sb", [P, D])
        woT = sb("woT", [P, D])
        MT = sb("MT", [P, P])
        WVO = sb("WVO", [P, D])
        gx = sb("gx", [P, 1])
        gf = sb("gf", [P, 1])
        tgx = sb("tgx", [P, 1])
        tgf = sb("tgf", [P, 1])
        bo = sb("bo", [P, D])
        gamma = sb("gamma", [P, 1])
        beta = sb("beta", [P, 1])
        w1n = sb("w1n", [P, NE, FB, D])
        w2n = sb("w2n", [P, NE, F])
        wabs = sb("wabs", [P, NE, FB])
        half = sb("half", [P, NE, FB])
        nhalf = sb("nhalf", [P, NE, FB])
        wabs2 = sb("wabs2", [P, NE])
        half2 = sb("half2", [P, NE])
        nhalf2 = sb("nhalf2", [P, NE])
        work = sb("work", [P, NE * F])
        neg1 = work[:].rearrange("p (e b d) -> p e b d", e=NE, b=FB)
        W1T = sb("W1T", [P, NE, FB, P], BF16)
        W2T = sb("W2T", [P, NE, FB, P])
        rw = sb("rw", [E, D])
        carrier = sb("carrier", [P, 1])
        act_carrier = sb("act_carrier", [P, 1])
        RWT = sb("RWT", [P, E])
        st = sb("st", [P, B, 6])
        mv = sb("mv", [P, B, 2])
        ve = sb("ve", [P, B])
        sd = sb("sd", [P, B])
        rstd = sb("rstd", [P, B])
        nmr = sb("nmr", [P, B])
        xn = sb("xn", [P, QB, D])
        xT = [sb(f"xT_{w}", [P, 2, QB * P], FP32R) for w in ("hi", "lo")]
        ctxT = sb("ctxT", [P, QB * SK])
        kp = [sb(f"kp_{w}", [P, QB * SK]) for w in ("hi", "lo")]
        kbd = [sb(f"kbd_{w}", [P, 2, QB, GH, SK], FP32R) for w in ("hi", "lo")]
        vm = sb("vm", [SK, 2, G, GH, GR])
        mx = sb("mx", [P, 2, 2, GH])
        nm = sb("nm", [P, 2, P])
        mT = sb("mT", [P, 2, P], FP32R)
        prob = sb("prob", [P, 2, 2, 2, GH, SP])
        part = sb("part", [P, H, SP // 2])
        shared = sb("shared", [P, 2 * H * P])
        PT = shared[0:SK, :].rearrange("p (s g c) -> p s g c", s=2, g=G)
        rsum = sb("rsum", [P, 2, H])
        rinv = sb("rinv", [P, 2, H, HD])
        rrec = sb("rrec", [P, H])
        rspread = sb("rspread", [P, P])
        oT = sb("oT", [P, P])
        lg = sb("lg", [P, B, E])
        lmax = sb("lmax", [P, B])
        eq = sb("eq", [P, B, E])
        rank = sb("rank", [P, E])
        best = sb("best", [P, B])
        gate = sb("gate", [P, B, E])
        topp = sb("topp", [P, B])
        hq = shared[:, 0:2 * BANK].rearrange("p (s c) -> p s c", s=2)
        xn2 = shared[:, 2 * BANK:4 * BANK].rearrange("p (s b d) -> p s b d", s=2, b=QB)
        trib = sb("trib", [P, P], BF16)
        onesb = sb("onesb", [P, P], BF16)
        eqb = sb("eqb", [P, B, E], BF16)
        region0 = sb("region0", [P, NE])
        num = sb("num", [P, NT])
        num_i = sb("num_i", [P, NT], I32)
        pnum = sb("pnum", [P, 1])
        pnum_i = sb("pnum_i", [P, 1], I32)
        tok_i = sb("tok_i", [P, B], I32)
        scan = sb("scan", [P, 2, B, E])
        pos = sb("pos", [P, B])
        pos_i = sb("pos_i", [P, B], I32)
        tiles_of = sb("tiles_of", [P, 3, E])
        gap = sb("gap", [P, E])
        cmp_k = sb("cmp_k", [P, E, TOKENS // P])
        cmp_t = sb("cmp_t", [P, NT, E])
        tile_f = sb("tile_f", [P, NT])
        tile_e = sb("tile_e", [P, NT], I32)
        tile_row = sb("tile_row", [P, NT], I32)
        pad_f = sb("pad_f", [P, NE])
        pad_i = sb("pad_i", [P, NE], I32)
        pad_row = sb("pad_row", [P, ROW])
        pay = prob[:].rearrange("p a b c d e -> p (a b c d e)")[:, 0:PAYS * QB * ROW].rearrange("p (s b r) -> p s b r", s=PAYS, b=QB)
        pay_i = sb("pay_i", [P, PAYS, QB], I32)
        tin = sb("tin", [P, SLOTS, 2, ROW])
        xh = sb("xh", [P, 2, 2, D])
        hT = sb("hT", [P, 2, 2 * P])
        rest = sb("rest", [P, 2 * P])
        hpart = sb("hpart", [P, 2, 3, 2 * P], BF16)
        h1s = shared[:, 0:4 * F].rearrange("p (s f c) -> p s f c", s=2, f=FB)
        h1r = shared[:, 4 * F:8 * F].rearrange("p (s a f c) -> p s a f c", s=2, a=2, f=FB)
        res = sb("res", [P, SLOTS, 2, D])

        x_in = [sem(f"x_in{c}") for c in range(XC)]
        w_in, ffw_in = sem("w_in"), sem("ffw_in")
        ctx_in = [sem("ctx_in0"), sem("ctx_in1")]
        pool_c, dve_c = sem("pool_step"), sem("dve_step")
        consts_ready, var_ready, sd_ready, stats_ready = (sem(x) for x in ("consts_ready", "var_ready", "sd_ready", "stats_ready"))
        tanh_ready, bd_ready, wo_psum, wo_copied = (sem(x) for x in ("tanh_ready", "bd_ready", "wo_psum", "wo_copied"))
        wvo_psum, quantised, wT_psum, wT_copied = (sem(x) for x in ("wvo_psum", "quantised", "wT_psum", "wT_copied"))
        xb_ready, var2_ready, top_ready, gexp_ready, hT_kept = (sem(x) for x in ("xb_ready", "var2_ready", "top_ready", "gexp_ready", "hT_kept"))
        xn_ready, vm_ready = sem("xn_ready"), sem("vm_ready")
        prep_psum, prep_copied = sem("prep_psum"), sem("prep_copied")
        scores_ready, max_ready = sem("scores_ready"), sem("max_ready")
        mt_psum, mt_copied = sem("mt_psum"), sem("mt_copied")
        shifted, exp_done = sem("shifted"), sem("exp_done")
        pt_psum = [sem("pt_psum0"), sem("pt_psum1")]
        pt_copied = [sem("pt_copied0"), sem("pt_copied1")]
        pv_done, o_ready, proj_done, x1_done = sem("pv_done"), sem("o_ready"), sem("proj_done"), sem("x1_done")
        spread_psum, spread_copied = sem("spread_psum"), sem("spread_copied")
        x1_stats, kp_copied, kbd_ready = sem("x1_stats"), sem("kp_copied"), sem("kbd_ready")
        mx_done, hi_done, part_step, part_done = sem("mx_done"), sem("hi_done"), sem("part_step"), sem("part_done")
        rsum_done, rinv_done, xhi_done, hr_hi, hr_lo = (sem(x) for x in ("rsum_done", "rinv_done", "xhi_done", "hr_hi", "hr_lo"))
        h_ready, hT_psum, hT_copied, logits_done = sem("h_ready"), sem("hT_psum"), sem("hT_copied"), sem("logits_done")
        eq_ready, ranks_psum, pos_ready, tables_ready = (sem(x) for x in ("eq_ready", "ranks_psum", "pos_ready", "tables_ready"))
        pay_ready = sem("pay_ready")
        rw_psum, rw_copied = sem("rw_psum"), sem("rw_copied")
        sorted_out = [sem(f"sorted_out{k}") for k in range(PAYS)]
        pads_out, carried, act_carried = sem("pads_out"), sem("carried"), sem("act_carried")
        tile_in = [sem(f"tile_in{k}") for k in range(SLOTS)]
        xh_ready, tileT_psum, tileT_copied, h_part, split_done = (sem(x) for x in ("xh_ready", "tileT_psum", "tileT_copied", "h_part", "split_done"))
        zs_psum, zr_psum, silu_done, y_psum, y_sum, res_ready = (sem(x) for x in ("zs_psum", "zr_psum", "silu_done", "y_psum", "y_sum", "res_ready"))
        rrec_done = sem("rrec_done")
        out_done = [sem(f"out_done{k}") for k in range(SLOTS)]

        block = ctx.enter_context(nc.Block())
        N_W = 8 + 3

        @block.sync
        def _(sp):
            for c in range(XC):
                n = B // XC
                sp.dma_start(X[:, c * n:(c + 1) * n, :],
                             A["x"][c * n:(c + 1) * n].rearrange("b q d -> q b d")).then_inc(x_in[c], 16)

            def load_ctx(q, s):
                ge(sp, vm_ready, QB * (q - 1))
                ge(sp, prep_psum, 3 * (q - 2) + 2)
                sp.dma_start(ctxq[:, s], A["ctx"][bass.ds(q * QB, QB)].rearrange("b k d -> k b d")).then_inc(ctx_in[s], 16)

            load_ctx(0, 0)
            load_ctx(1, 1)
            with sp.Fori(0, (NQ - 2) // 2) as i2:
                load_ctx(2 * i2 + 2, 0)
                load_ctx(2 * i2 + 3, 1)
            for k in range(PAYS):
                sp.wait_ge(sorted_out[k], 16 * B // PAYS)
            sp.wait_ge(pads_out, 16 * NE)

            def group(g, first=False):
                for k in range(SLOTS):
                    if not first:
                        sp.wait_ge(out_done[k], 32 * g)
                    for a in range(2):
                        row = sp.value_load(tile_row[0:1, bass.ds((g * SLOTS + k) * 2 + a, 1)], min_val=0, max_val=E * REGION)
                        sp.dma_start(tin[:, k, a, :], A["rows"][bass.ds(row, P), :]).then_inc(tile_in[k], 16)

            group(0, True)
            with sp.Fori(0, NG - 1) as gi:
                group(gi + 1)
            for k in range(SLOTS):
                sp.wait_ge(out_done[k], 32 * NG)

        @block.gpsimd
        def _(pool):
            n = [0]

            def step(ins):
                n[0] += 1
                ins.then_inc(pool_c, 1)
                pool.wait_ge(pool_c, n[0])

            def band(t, pattern, base_lo, base_hi, cm):
                step(nc.gpsimd.affine_select(out=t, in_=t, compare_op=ALU.is_ge, fill=0.0, base=base_lo,
                                             pattern=pattern, channel_multiplier=cm))
                step(nc.gpsimd.affine_select(out=t, in_=t, compare_op=ALU.is_ge, fill=0.0, base=base_hi,
                                             pattern=[[-s, c] for s, c in pattern], channel_multiplier=-cm))

            step(nc.gpsimd.memset(ident[:], 0.0))
            step(nc.gpsimd.affine_select(out=ident[:], in_=ident[:], compare_op=ALU.not_equal, fill=1.0,
                                         base=0, pattern=[[-1, P]], channel_multiplier=1))
            step(nc.gpsimd.memset(headsel[:], 1.0))
            band(headsel[:], [[-HD, H], [0, HD]], 0, HD - 1, 1)
            step(nc.gpsimd.memset(vm[:], 0.0))
            step(nc.gpsimd.memset(ones[:], 1.0))
            step(nc.gpsimd.memset(nm[:], 0.0))
            step(nc.gpsimd.memset(prob[:], 0.0))
            for i in range(E):
                step(nc.gpsimd.memset(rank[:, i:i + 1], float(E - i)))
            step(nc.gpsimd.tensor_tensor(rowsel[:], headsel[:, 0:GH, 0], headsel[:, GH:2 * GH, 0], ALU.add))
            for g in range(2, G):
                step(nc.gpsimd.tensor_tensor(rowsel[:], rowsel[:], headsel[:, g * GH:(g + 1) * GH, 0], ALU.add))
            step(nc.gpsimd.tensor_tensor(shiftsel[:], ident[:, 0:GH], ident[:, GR:GR + GH], ALU.add))
            for g in range(2, G):
                step(nc.gpsimd.tensor_tensor(shiftsel[:], shiftsel[:], ident[:, g * GR:g * GR + GH], ALU.add))
            for g in range(G):
                step(nc.gpsimd.tensor_tensor(shiftsel[:], shiftsel[:], ident[:, g * GR + GH:g * GR + 2 * GH], ALU.add))
            step(nc.gpsimd.tensor_copy(ind[:], shiftsel[:].unsqueeze(2).broadcast_to([P, GH, SK])))
            step(nc.gpsimd.tensor_copy(identb[:], ident[:]))
            step(nc.gpsimd.memset(onesb[:], 1.0))
            step(nc.gpsimd.affine_select(out=trib[:], in_=onesb[:], compare_op=ALU.is_ge, fill=0.0, base=-1,
                                         pattern=[[1, P]], channel_multiplier=-1))
            for i in range(NE):
                step(nc.gpsimd.memset(region0[:, i:i + 1], float(i * REGION)))
            step(nc.gpsimd.iota(num_i[:], pattern=[[1, NT]], base=0, channel_multiplier=0))
            step(nc.gpsimd.tensor_copy(num[:], num_i[:]))
            step(nc.gpsimd.iota(pnum_i[:], pattern=[[0, 1]], base=0, channel_multiplier=1))
            step(nc.gpsimd.tensor_copy(pnum[:], pnum_i[:]))
            step(nc.gpsimd.iota(tok_i[:], pattern=[[SQ, B]], base=0, channel_multiplier=1))
            step(nc.gpsimd.memset(pad_row[:], 0.0))
            step(nc.gpsimd.memset(pad_row[:, ROW - 1:ROW].bitcast(I32), TOKENS))
            pool.sem_inc(consts_ready, 1)

            pool.wait_ge(bd_ready, 1)

            def own_columns(v):
                return bass.AP(v.tensor, v.offset, [list(v.ap[0]), [GH * GR, G], [GR + HD, GH], [1, HD]])

            def make_vm(b, j, s):
                ge(pool, pv_done, b - 1)
                nc.gpsimd.tensor_tensor(own_columns(vm[:, j % 2]),
                                        ctxq[:, s, j, :].rearrange("k (g i c) -> k g i c", g=G, i=GH),
                                        ones[0:SK, 0:P].rearrange("k (g i c) -> k g i c", g=G, i=GH),
                                        ALU.mult).then_inc(vm_ready, 1)
                xb = X[:, bass.ds(b, 1), :].squeeze(1)
                nc.gpsimd.tensor_tensor(xb, xb, bo[:], ALU.add).then_inc(xb_ready, 1)

            def expand_keys(b, q, s, j):
                pool.wait_ge(kp_copied, 2 * (q + 1))
                for w in range(2):
                    ins = nc.gpsimd.tensor_tensor(
                        kbd[w][:, s, j], kp[w][:, j * SK:(j + 1) * SK].unsqueeze(1).broadcast_to([P, GH, SK]),
                        rowsel[:].unsqueeze(2).broadcast_to([P, GH, SK]), ALU.mult)
                ins.then_inc(kbd_ready, 1)

            def add_probs(b, s):
                pool.wait_ge(exp_done, 2 * b + 2)
                ge(pool, rsum_done, b)
                p = prob[:, s].rearrange("p u v i k -> p (u v i) k")
                m = SP // 2
                nc.gpsimd.tensor_tensor(part[:], p[:, :, 0:m], p[:, :, m:SP], ALU.add).then_inc(part_step, 1)
                pool.wait_ge(part_step, 2 * b + 1)
                nc.gpsimd.tensor_tensor(part[:, :, 0:RN], part[:, :, 0:RN], part[:, :, RN:2 * RN], ALU.add).then_inc(part_step, 1)
                pool.wait_ge(part_step, 2 * b + 2)
                nc.gpsimd.tensor_tensor(part[:, :, 0:RN], part[:, :, 0:RN], part[:, :, 2 * RN:3 * RN], ALU.add).then_inc(part_done, 1)

            def quad(q, s, arrived, last=False):
                pool.wait_ge(xn_ready, q + 1)
                pool.wait_ge(ctx_in[s], 16 * arrived)
                for j in range(QB):
                    b = q * QB + j
                    if not (isinstance(b, int) and b == 0):
                        add_probs(b - 1, (j - 1) % 2)
                    if j < QB - 1:
                        expand_keys(b + 1, q, s, j + 1)
                    elif not last:
                        expand_keys(b + 1, q + 1, 1 - s, 0)
                    make_vm(b, j, s)

            expand_keys(0, 0, 0, 0)

            quad(0, 0, 1)
            with pool.Fori(0, (NQ - 2) // 2) as i2:
                quad(2 * i2 + 1, 1, i2 + 1)
                quad(2 * i2 + 2, 0, i2 + 2)
            quad(NQ - 1, 1, NQ // 2, last=True)
            add_probs(B - 1, 1)

            def carry(n):
                pool.wait_ge(carried, n + 1)
                nc.gpsimd.tensor_tensor(carrier[:], rank[:, 0:1], rank[:, 0:1], ALU.add).then_inc(carried, 1)

            nc.gpsimd.memset(carrier[:], 0.0).then_inc(carried, 1)
            def row_of(idx):
                return bass.IndirectOffsetOnAxis(ap=idx.bitcast(mybir.dt.uint32), axis=0)

            def sort_quad(q, s):
                pool.wait_ge(pay_ready, q + 1)
                carry(q)
                for j in range(QB):
                    nc.gpsimd.indirect_dma_start(out=A["rows"][:, :], out_offset=row_of(pay_i[:, s, j:j + 1]),
                                                 in_=pay[:, s, j, :], in_offset=None).then_inc(sorted_out[s], 16)

            with pool.Fori(0, NQ // PAYS) as i4:
                for s in range(PAYS):
                    sort_quad(PAYS * i4 + s, s)
            pool.wait_ge(tables_ready, 1)
            for e in range(NE):
                nc.gpsimd.indirect_dma_start(out=A["rows"][:, :], out_offset=row_of(pad_i[:, e:e + 1]),
                                             in_=pad_row[:], in_offset=None).then_inc(pads_out, 16)

            def group(g):
                for k in range(SLOTS):
                    pool.wait_ge(res_ready, g * SLOTS + k + 1)
                    carry(NQ + g * SLOTS + k)
                    for a in range(2):
                        nc.gpsimd.indirect_dma_start(out=A["out"].rearrange("b q d -> (b q) d"),
                                                     out_offset=row_of(tin[:, k, a, ROW - 1:ROW]),
                                                     in_=res[:, k, a, :], in_offset=None,
                                                     bounds_check=TOKENS - 1, oob_is_err=False).then_inc(out_done[k], 16)

            with pool.Fori(0, NG) as gi:
                group(gi)

        @block.vector
        def _(dve):
            n = [0]

            def step(ins, signal=None):
                if signal is not None:
                    ins.then_inc(signal, 1)
                    dve.wait_ge(signal, 1)
                    return
                n[0] += 1
                ins.then_inc(dve_c, 1)
                dve.wait_ge(dve_c, n[0])

            def newton(v, inv):
                step(nc.vector.tensor_tensor(sd[:], inv, inv, ALU.mult))
                step(nc.vector.tensor_tensor(sd[:], sd[:], v, ALU.mult))
                step(nc.vector.tensor_scalar(sd[:], sd[:], -0.5, 1.5, ALU.mult, ALU.add))
                step(nc.vector.tensor_tensor(inv, inv, sd[:], ALU.mult))

            for b in range(B):
                if b % (B // XC) == 0:
                    dve.wait_ge(x_in[b // (B // XC)], 16)
                ins = nc.vector.bn_stats(st[:, b, :], X[:, b, :])
            step(ins)

            dve.wait_ge(w_in, 16 * N_W)
            dve.wait_ge(consts_ready, 1)
            for bd, w in ((wq_bd, wq8), (wk_bd, wk8), (wv_bd, wv8)):
                ins = nc.vector.tensor_tensor(bd[:], w[:].unsqueeze(1).broadcast_to([P, H, HD]), headsel[:], ALU.mult)
            step(ins)
            dve.wait_ge(tanh_ready, 1)
            step(nc.vector.tensor_scalar(bo[:], bo[:], tgx[:], None, ALU.mult), bd_ready)
            for b in range(B):
                ins = nc.vector.bn_aggr(mv[:, b, :], st[:, b, :])
            step(ins)
            step(nc.vector.tensor_scalar(ve[:], mv[:, :, 1], EPS, None, ALU.add), var_ready)
            dve.wait_ge(wo_psum, 1)
            step(nc.vector.tensor_copy(woT[:], PS[:, 0, 0:P]))
            step(nc.vector.tensor_copy(MT[:], PS[:, 1, 0:P]), wo_copied)
            dve.wait_ge(sd_ready, 1)
            step(nc.vector.reciprocal(rstd[:], sd[:]))
            newton(ve[:], rstd[:])
            step(nc.vector.scalar_tensor_tensor(nmr[:], mv[:, :, 0], -1.0, rstd[:], ALU.mult, ALU.mult), stats_ready)
            step(nc.vector.tensor_scalar(maskneg[:], mask_i[:].unsqueeze(1).broadcast_to([P, GH, SK]), 0.0, MASKED,
                                         ALU.is_equal, ALU.mult))
            dve.wait_ge(wvo_psum, 1)
            step(nc.vector.tensor_scalar(WVO[:], PS[:, 0, 0:D], tgx[:], None, ALU.mult))
            dve.wait_ge(rw_psum, 1)
            step(nc.vector.tensor_copy(RWT[:], PS[:, 4, 0:E]), rw_copied)

            def prep_x(q, qs):
                dve.wait_ge(xhi_done, q + 1)
                nc.vector.tensor_tensor(xT[1][:, qs], PS[:, 6, :], xT[0][:, qs].bitcast(FP32), ALU.subtract).then_inc(prep_copied, 1)

            def prep_k(q):
                dve.wait_ge(kp_copied, 2 * q + 1)
                nc.vector.tensor_tensor(kp[1][:], PS[:, 6, 0:QB * SK], kp[0][:], ALU.subtract).then_inc(kp_copied, 1)

            def take_max(b, u):
                dve.wait_ge(scores_ready, 2 * b + u + 1)
                nc.vector.tensor_reduce(mx[:, u], PS[:, 2 * u:2 * u + 2, 0:GK].rearrange("p g (i k) -> p g i k", k=SK),
                                        AX.X, ALU.max, negate=True).then_inc(mx_done, 1)
                ge(dve, mt_psum, 2 * (b - 1) + u + 1)
                dve.wait_ge(mx_done, 2 * b + u + 1)
                cols = nm[:, u, :].rearrange("p (g r) -> p g r", g=G)[:, 2 * u:2 * u + 2]
                nc.vector.tensor_copy(cols[:, :, 0:GH].bitcast(FP32R), mx[:, u]).then_inc(hi_done, 1)
                dve.wait_ge(hi_done, 2 * b + u + 1)
                nc.vector.tensor_tensor(cols[:, :, GH:2 * GH], mx[:, u], cols[:, :, 0:GH], ALU.subtract).then_inc(max_ready, 1)

            def copy_pt(b, s, u):
                dve.wait_ge(pt_psum[1], 2 * b + u + 1)
                ge(dve, pv_done, b - 1)
                nc.vector.tensor_copy(PT[:, s, 2 * u + 1, :], PS[0:SK, 5, :]).then_inc(pt_copied[1], 1)

            def sums(b, s):
                dve.wait_ge(part_done, b + 1)
                nc.vector.tensor_reduce(rsum[:, s], part[:, :, 0:RN], AX.X, ALU.add).then_inc(rsum_done, 1)
                dve.wait_ge(rsum_done, b + 1)
                nc.vector.reciprocal(rrec[:], rsum[:, s]).then_inc(rrec_done, 1)
                dve.wait_ge(rrec_done, b + 1)
                nc.vector.tensor_copy(rinv[:, s], rrec[:].unsqueeze(2).broadcast_to([P, H, HD])).then_inc(rinv_done, 1)

            def normalise(b):
                dve.wait_ge(pv_done, b + 1)
                dve.wait_ge(spread_copied, b + 1)
                nc.vector.tensor_tensor(oT[:], PS[:, 7, 0:P], rspread[:], ALU.mult).then_inc(o_ready, 1)

            def residual(b):
                dve.wait_ge(proj_done, b + 1)
                dve.wait_ge(xb_ready, b + 1)
                xb = X[:, bass.ds(b, 1), :].squeeze(1)
                nc.vector.tensor_tensor(xb, xb, PS[:, 7, 2 * P:3 * P], ALU.add).then_inc(x1_done, 1)
                dve.wait_ge(x1_done, b + 1)
                nc.vector.bn_stats(st[:, bass.ds(b, 1), :].squeeze(1), xb).then_inc(x1_stats, 1)

            prep_x(0, 0)
            prep_k(0)

            def step_of(b, s, j, front, mid, back, q=None, q2=None, prep=False):
                if front:
                    take_max(b, 0)
                if mid:
                    copy_pt(b - 1, 1 - s, 0)
                if front:
                    take_max(b, 1)
                if mid:
                    copy_pt(b - 1, 1 - s, 1)
                    sums(b - 1, 1 - s)
                if back:
                    normalise(b - 2)
                if prep and j == 0:
                    prep_x(q + 1, 1 - q2)
                if prep and j == 2:
                    prep_k(q + 1)
                if back:
                    residual(b - 2)

            def quad(q, q2, last=False):
                for j in range(QB):
                    b = q * QB + j
                    at = b if isinstance(b, int) else 2
                    step_of(b, j % 2, j, True, at >= 1, at >= 2, q, q2, not last)

            quad(0, 0)
            with dve.Fori(0, (NQ - 2) // 2) as i2:
                quad(2 * i2 + 1, 1)
                quad(2 * i2 + 2, 0)
            quad(NQ - 1, 1, last=True)
            step_of(B, 0, 0, False, True, True)
            step_of(B + 1, 1, 1, False, False, True)

            dve.wait_ge(x1_stats, B)
            for b in range(B):
                ins = nc.vector.bn_aggr(mv[:, b, :], st[:, b, :])
            step(ins)
            step(nc.vector.tensor_scalar(ve[:], mv[:, :, 1], 1.0 + EPS, EPS * EPS, ALU.mult, ALU.add), var2_ready)
            dve.wait_ge(sd_ready, 2)
            step(nc.vector.reciprocal(rstd[:], sd[:]))
            newton(ve[:], rstd[:])
            step(nc.vector.scalar_tensor_tensor(nmr[:], mv[:, :, 0], -1.0, rstd[:], ALU.mult, ALU.mult))
            def make_h(q, s):
                ge(dve, hT_psum, q - 1)
                for j in range(QB):
                    b = q * QB + j
                    ins = nc.vector.tensor_scalar(xn2[:, s, j, :], X[:, bass.ds(b, 1), :].squeeze(1),
                                                  rstd[:, bass.ds(b, 1)], nmr[:, bass.ds(b, 1)], ALU.mult, ALU.add)
                ins.then_inc(h_ready, 1)

            for s in range(2):
                make_h(s, s)
            with dve.Fori(0, NQ // 2 - 1) as i2:
                for s in range(2):
                    make_h(2 * i2 + 2 + s, s)
            dve.wait_ge(logits_done, NQ)
            lgp = PS[:, 4, :].rearrange("p (b e) -> p b e", e=E)
            step(nc.vector.tensor_reduce(lmax[:], lgp, AX.X, ALU.max))
            step(nc.vector.tensor_tensor(lg[:], lgp, lmax[:].unsqueeze(2).broadcast_to([P, B, E]), ALU.subtract))
            step(nc.vector.tensor_scalar(eq[:], lg[:], 0.0, None, ALU.is_equal))
            step(nc.vector.tensor_tensor(eq[:], eq[:], rank[:].unsqueeze(1).broadcast_to([P, B, E]), ALU.mult))
            step(nc.vector.tensor_reduce(best[:], eq[:], AX.X, ALU.max))
            step(nc.vector.tensor_tensor(eq[:], eq[:], best[:].unsqueeze(2).broadcast_to([P, B, E]), ALU.is_equal), top_ready)
            step(nc.vector.tensor_copy(eqb[:], eq[:]), eq_ready)
            dve.wait_ge(gexp_ready, 1)
            step(nc.vector.tensor_reduce(topp[:], gate[:], AX.X, ALU.add))
            step(nc.vector.reciprocal(topp[:], topp[:]))
            dve.wait_ge(ranks_psum, 1)
            cum = PS[:, 0, :].rearrange("p (b e) -> p b e", e=E)
            tot = PS[:, 1, :].rearrange("p (b e) -> p b e", e=E)
            step(nc.vector.tensor_copy(scan[:, 0], tot))
            c, shift_by = 0, 1
            while shift_by < B:
                nc.vector.tensor_copy(scan[:, 1 - c, 0:shift_by], scan[:, c, 0:shift_by])
                step(nc.vector.tensor_tensor(scan[:, 1 - c, shift_by:B], scan[:, c, shift_by:B],
                                             scan[:, c, 0:B - shift_by], ALU.add))
                c, shift_by = 1 - c, 2 * shift_by
            counts = scan[:, c, B - 1, :]
            w = scan[:, 1 - c]
            step(nc.vector.tensor_tensor(w, scan[:, c], tot, ALU.subtract))
            step(nc.vector.tensor_tensor(w, w, cum, ALU.add))
            step(nc.vector.tensor_tensor(w, w, region0[:, 0:E].unsqueeze(1).broadcast_to([P, B, E]), ALU.add))
            step(nc.vector.tensor_tensor(w, w, eq[:], ALU.mult))
            step(nc.vector.tensor_reduce(pos[:], w, AX.X, ALU.add))
            step(nc.vector.tensor_copy(pos_i[:], pos[:]), pos_ready)

            step(nc.vector.tensor_scalar(tile_f[:], num[:], float(P), None, ALU.mult))
            step(nc.vector.tensor_tensor(cmp_k[:], counts.unsqueeze(2).broadcast_to([P, E, TOKENS // P]),
                                         tile_f[:, 0:TOKENS // P].unsqueeze(1).broadcast_to([P, E, TOKENS // P]), ALU.is_gt))
            step(nc.vector.tensor_reduce(tiles_of[:, 0], cmp_k[:], AX.X, ALU.add))
            step(nc.vector.tensor_scalar(gap[:], tiles_of[:, 0], -float(P), float(REGION), ALU.mult, ALU.add))
            step(nc.vector.tensor_copy(tiles_of[:, 1], tiles_of[:, 0]))
            c, shift_by = 1, 1
            while shift_by < E:
                nc.vector.tensor_copy(tiles_of[:, 3 - c, 0:shift_by], tiles_of[:, c, 0:shift_by])
                step(nc.vector.tensor_tensor(tiles_of[:, 3 - c, shift_by:E], tiles_of[:, c, shift_by:E],
                                             tiles_of[:, c, 0:E - shift_by], ALU.add))
                c, shift_by = 3 - c, 2 * shift_by
            step(nc.vector.tensor_tensor(cmp_t[:], num[:].unsqueeze(2).broadcast_to([P, NT, E]),
                                         tiles_of[:, c].unsqueeze(1).broadcast_to([P, NT, E]), ALU.is_ge))
            step(nc.vector.tensor_reduce(tile_f[:], cmp_t[:], AX.X, ALU.add))
            step(nc.vector.tensor_scalar(tile_e[:], tile_f[:], float(E - 1), None, ALU.min))
            step(nc.vector.tensor_tensor(cmp_t[:], cmp_t[:], gap[:].unsqueeze(1).broadcast_to([P, NT, E]), ALU.mult))
            step(nc.vector.tensor_reduce(tile_f[:], cmp_t[:], AX.X, ALU.add))
            step(nc.vector.scalar_tensor_tensor(tile_f[:], num[:], float(P), tile_f[:], ALU.mult, ALU.add))
            step(nc.vector.tensor_scalar(tile_row[:], tile_f[:], float(E * REGION), None, ALU.min))
            nc.vector.tensor_copy(pad_f[:, E:NE], region0[:, E:NE])
            step(nc.vector.tensor_tensor(pad_f[:, 0:E], counts, region0[:, 0:E], ALU.add))
            step(nc.vector.tensor_scalar(pad_i[:], pad_f[:], pnum[:], None, ALU.add), tables_ready)

            dve.wait_ge(ffw_in, 16 * 4)
            step(nc.vector.tensor_reduce(wabs[:], w1n[:], AX.X, ALU.add, apply_absolute_value=True))
            step(nc.vector.tensor_reduce(wabs2[:], w2n[:], AX.X, ALU.add, apply_absolute_value=True))
            step(nc.vector.tensor_scalar(wabs[:], wabs[:], 1.0 / D, 1e-5, ALU.mult, ALU.max))
            step(nc.vector.tensor_scalar(wabs2[:], wabs2[:], 1.0 / F, 1e-5, ALU.mult, ALU.max))
            for s, hh, nh in ((wabs, half, nhalf), (wabs2, half2, nhalf2)):
                step(nc.vector.tensor_scalar(hh[:], s[:], 0.5, None, ALU.mult))
                step(nc.vector.tensor_scalar(nh[:], s[:], -0.5, None, ALU.mult))
            step(nc.vector.tensor_scalar(wabs2[:], wabs2[:], tgf[:], None, ALU.mult))

            def quantise(w, s, hh, nh, neg, signal=None):
                shape = list(w.shape)
                step(nc.vector.tensor_tensor(neg, w, nh.broadcast_to(shape), ALU.is_lt))
                step(nc.vector.tensor_tensor(w, w, hh.broadcast_to(shape), ALU.is_gt))
                step(nc.vector.tensor_tensor(w, w, neg, ALU.subtract))
                if s is not None:
                    step(nc.vector.tensor_tensor(w, w, s.broadcast_to(shape), ALU.mult), signal)

            quantise(w1n[:], None, half[:].unsqueeze(3), nhalf[:].unsqueeze(3), neg1)
            quantise(w2n[:], wabs2[:].unsqueeze(2), half2[:].unsqueeze(2), nhalf2[:].unsqueeze(2),
                     neg1.rearrange("p e b d -> p e (b d)"), quantised)
            for e in range(NE):
                dve.wait_ge(wT_psum, e + 1)
                nc.vector.tensor_copy(W1T[:, e], PS[:, 2 * (e % 2), 0:F])
                nc.vector.tensor_copy(W2T[:, e], PS[:, 2 * (e % 2) + 1, 0:F]).then_inc(wT_copied, 1)

            def normalise_tile(g, k):
                n = g * SLOTS + k
                dve.wait_ge(tile_in[k], 32 * (g + 1))
                ge(dve, tileT_psum, n - 1)
                for a in range(2):
                    ins = nc.vector.tensor_scalar(xh[:, k % 2, a], tin[:, k, a, 0:D], tin[:, k, a, D:D + 1],
                                                  tin[:, k, a, D + 1:D + 2], ALU.mult, ALU.add)
                ins.then_inc(xh_ready, 1)

            def split(g, k):
                n = g * SLOTS + k
                s = k % 2
                dve.wait_ge(tileT_copied, n + 1)
                ge(dve, zr_psum, n - 1)
                for part_, (src, to) in enumerate(((hT[:, s], rest[:]), (rest[:], hpart[:, s, 2]))):
                    nc.vector.tensor_copy(hpart[:, s, part_], src).then_inc(h_part, 1)
                    dve.wait_ge(h_part, 3 * n + 2 * part_ + 1)
                    ins = nc.vector.tensor_tensor(to, src, hpart[:, s, part_], ALU.subtract)
                    if part_ == 0:
                        ins.then_inc(h_part, 1)
                        dve.wait_ge(h_part, 3 * n + 2)
                ins.then_inc(split_done, 1)

            def combine(g, k):
                n = g * SLOTS + k
                dve.wait_ge(y_psum, n + 1)
                y = PS[:, 4 + k % 2, :].rearrange("p (a w d) -> p a w d", a=2, w=2)
                nc.vector.tensor_tensor(res[:, k], tin[:, k, :, 0:D], y[:, :, 0], ALU.add).then_inc(y_sum, 1)
                dve.wait_ge(y_sum, n + 1)
                for a in range(2):
                    ins = nc.vector.scalar_tensor_tensor(res[:, k, a], y[:, a, 1], tin[:, k, a, D + 2:D + 3], res[:, k, a],
                                                         ALU.mult, ALU.add)
                ins.then_inc(res_ready, 1)

            normalise_tile(0, 0)
            normalise_tile(0, 1)
            split(0, 0)

            def group(g, first=False, last=False):
                for k in range(SLOTS):
                    if k < SLOTS - 2:
                        normalise_tile(g, k + 2)
                    elif not last:
                        normalise_tile(g + 1, k + 2 - SLOTS)
                    if k < SLOTS - 1:
                        split(g, k + 1)
                    elif not last:
                        split(g + 1, 0)
                    if k > 0:
                        combine(g, k - 1)
                    elif not first:
                        combine(g - 1, SLOTS - 1)

            group(0, first=True)
            with dve.Fori(0, NG - 2) as gi:
                group(gi + 1)
            group(NG - 1, last=True)
            combine(NG - 1, SLOTS - 1)

        @block.scalar
        def _(act):
            act.dma_start(wo_sb[:], A["Wo"][:, :]).then_inc(w_in, 16)
            act.dma_start(mask_i[:], A["mask"][0, 0]).then_inc(w_in, 16)
            for t, name in ((wq8, "Wq"), (wk8, "Wk"), (wv8, "Wv")):
                w = A[name]
                act.dma_start(t[:], bass.AP(w.tensor, w.offset, [[0, H], [HD, HD], [1, HD]])).then_inc(w_in, 16)
            act.dma_start(gx[:], A["g_x"].unsqueeze(0).broadcast_to([P, 1])).then_inc(w_in, 16)
            act.dma_start(gf[:], A["g_f"].unsqueeze(0).broadcast_to([P, 1])).then_inc(w_in, 16)
            act.dma_start(bo[:], A["bo"].unsqueeze(0).broadcast_to([P, D])).then_inc(w_in, 16)
            act.dma_start(gamma[:], A["gamma"].unsqueeze(1)).then_inc(w_in, 16)
            act.dma_start(beta[:], A["beta"].unsqueeze(1)).then_inc(w_in, 16)
            act.dma_start(rw[:], A["rw"][:, :]).then_inc(w_in, 16)
            act.dma_start(w1n[:, 0:E], A["ew1"].rearrange("e (b p) d -> p e b d", p=P)).then_inc(ffw_in, 16)
            act.dma_start(w1n[:, E], A["sw1"].rearrange("(b p) d -> p b d", p=P)).then_inc(ffw_in, 16)
            act.dma_start(w2n[:, 0:E], A["ew2"].rearrange("e d f -> d e f")).then_inc(ffw_in, 16)
            act.dma_start(w2n[:, E], A["sw2"][:, :]).then_inc(ffw_in, 16)

            act.wait_ge(w_in, 16 * N_W)
            nc.scalar.activation(tgx[:], gx[:], ACT.Tanh)
            nc.scalar.activation(tgf[:], gf[:], ACT.Tanh).then_inc(tanh_ready, 1)
            act.wait_ge(var_ready, 1)
            nc.scalar.activation(sd[:], ve[:], ACT.Sqrt).then_inc(sd_ready, 1)

            def make_xn(q):
                for j in range(QB):
                    b = q * QB + j
                    ins = nc.scalar.activation(xn[:, j, :], X[:, bass.ds(b, 1), :].squeeze(1), ACT.Identity,
                                               bias=nmr[:, bass.ds(b, 1)], scale=rstd[:, bass.ds(b, 1)])
                ins.then_inc(xn_ready, 1)

            def prep_x(q, qs):
                act.wait_ge(prep_psum, 3 * q + 1)
                nc.scalar.copy(xT[0][:, qs], PS[:, 6, :]).then_inc(xhi_done, 1)

            def prep_ctx(q):
                act.wait_ge(prep_psum, 3 * q + 2)
                nc.scalar.copy(ctxT[:], PS[:, 6, 0:QB * SK]).then_inc(prep_copied, 1)

            def prep_k(q):
                act.wait_ge(prep_psum, 3 * q + 3)
                ge(act, kbd_ready, QB * q)
                nc.scalar.copy(kp[0][:].bitcast(FP32R), PS[:, 6, 0:QB * SK]).then_inc(kp_copied, 1)

            def copy_pt(b, s, u):
                act.wait_ge(pt_psum[0], 2 * b + u + 1)
                ge(act, pv_done, b - 1)
                nc.scalar.copy(PT[:, s, 2 * u, :], PS[0:SK, 4, :]).then_inc(pt_copied[0], 1)

            def copy_mt(b, u):
                act.wait_ge(mt_psum, 2 * b + u + 1)
                ge(act, shifted, 2 * (b - 1) + u + 1)
                nc.scalar.copy(mT[:, u, :], PS[:, 6, 0:P]).then_inc(mt_copied, 1)

            def copy_spread(b):
                act.wait_ge(spread_psum, b + 1)
                ge(act, o_ready, b)
                nc.scalar.copy(rspread[:], PS[:, 6, P:2 * P]).then_inc(spread_copied, 1)

            def exps(b, s, u):
                act.wait_ge(shifted, 2 * b + u + 1)
                for v in range(2):
                    ge(act, pt_psum[v], 2 * (b - 2) + u + 1)
                ge(act, part_done, b - 1)
                nc.scalar.activation(prob[:, s, u, :, :, 0:SK],
                                     PS[:, 2 * u:2 * u + 2, 0:GK].rearrange("p g (i k) -> p g i k", k=SK), ACT.Exp,
                                     scale=float(1.0 / np.sqrt(HD))).then_inc(exp_done, 1)

            act.wait_ge(stats_ready, 1)
            make_xn(0)
            prep_x(0, 0)
            prep_ctx(0)
            prep_k(0)

            def quad(q, q2, last=False):
                for j in range(QB):
                    b = q * QB + j
                    s = j % 2
                    first = isinstance(b, int) and b == 0
                    if not first:
                        copy_pt(b - 1, 1 - s, 0)
                    if j == 0 and not last:
                        make_xn(q + 1)
                    copy_mt(b, 0)
                    if not isinstance(b, int) or b >= 2:
                        copy_spread(b - 2)
                    if not first:
                        copy_pt(b - 1, 1 - s, 1)
                    exps(b, s, 0)
                    copy_mt(b, 1)
                    exps(b, s, 1)
                    if not last:
                        if j == 0:
                            prep_x(q + 1, 1 - q2)
                        elif j == 1:
                            prep_ctx(q + 1)
                        elif j == 2:
                            prep_k(q + 1)

            quad(0, 0)
            with act.Fori(0, (NQ - 2) // 2) as i2:
                quad(2 * i2 + 1, 1)
                quad(2 * i2 + 2, 0)
            quad(NQ - 1, 1, last=True)
            copy_pt(B - 1, 1, 0)
            copy_spread(B - 2)
            copy_pt(B - 1, 1, 1)
            copy_spread(B - 1)

            act.wait_ge(var2_ready, 1)
            nc.scalar.activation(sd[:], ve[:], ACT.Sqrt).then_inc(sd_ready, 1)
            def copy_h(q, s):
                act.wait_ge(hT_psum, q + 1)
                ge(act, logits_done, q - 1)
                nc.scalar.activation(hq[:, s], PS[:, 5 + s, :], ACT.Identity,
                                     bias=beta[:], scale=gamma[:]).then_inc(hT_copied, 1)

            for s in range(2):
                copy_h(s, s)
            with act.Fori(0, NQ // 2 - 1) as i2:
                for s in range(2):
                    copy_h(2 * i2 + 2 + s, s)
            act.wait_ge(top_ready, 1)
            nc.scalar.activation(gate[:], lg[:], ACT.Exp).then_inc(gexp_ready, 1)

            def fill_pay(q, s):
                quad_ = slice(q * QB, (q + 1) * QB) if isinstance(q, int) else bass.ds(q * QB, QB)
                nc.scalar.copy(pay[:, s, :, 0:D], X[:, quad_, :])
                for col, t in ((0, rstd), (1, nmr), (2, topp)):
                    nc.scalar.copy(pay[:, s, :, D + col:D + col + 1], t[:, quad_].unsqueeze(2))
                nc.scalar.copy(pay[:, s, :, D + 3:ROW].bitcast(I32), tok_i[:, quad_].unsqueeze(2))
                nc.scalar.copy(pay_i[:, s], pos_i[:, quad_]).then_inc(pay_ready, 1)

            nc.scalar.copy(act_carrier[:], gx[:]).then_inc(act_carried, 1)
            act.wait_ge(pos_ready, 1)
            for s in range(PAYS):
                fill_pay(s, s)
            with act.Fori(0, NQ // PAYS - 1) as i4:
                for s in range(PAYS):
                    act.wait_ge(sorted_out[s], 16 * QB * (i4 + 1))
                    act.wait_ge(act_carried, PAYS * i4 + s + 1)
                    nc.scalar.copy(act_carrier[:], gx[:]).then_inc(act_carried, 1)
                    fill_pay(PAYS * i4 + PAYS + s, s)

            def copy_tileT(g, k):
                n = g * SLOTS + k
                act.wait_ge(tileT_psum, n + 1)
                ge(act, split_done, n - 1)
                nc.scalar.activation(hT[:, k % 2], PS[:, 6, 0:2 * P], ACT.Identity,
                                     bias=beta[:], scale=gamma[:]).then_inc(tileT_copied, 1)

            def silus(g, k, experts):
                n = g * SLOTS + k
                s = k % 2
                act.wait_ge(zs_psum, n + 1)
                ge(act, y_psum, n - 1)
                for f in range(FB):
                    if f == 1:
                        act.wait_ge(zr_psum, n + 1)
                    nc.scalar.activation(h1s[:, s, f], PS[:, s, f * 2 * P:(f + 1) * 2 * P], ACT.Silu, scale=wabs[:, E, f:f + 1])
                for a in range(2):
                    for f in range(FB):
                        ins = nc.scalar.activation(h1r[:, s, a, f], PS[:, 2 + s, (2 * a + f) * P:(2 * a + f + 1) * P], ACT.Silu,
                                                   scale=wabs[:, bass.ds(experts[a], 1), f:f + 1].squeeze(1))
                ins.then_inc(silu_done, 1)

            act.wait_ge(tables_ready, 1)
            act.wait_ge(wT_copied, NE)
            copy_tileT(0, 0)

            def group(g, last=False):
                experts = nc.values_load_multi_w_load_instructions(
                    tile_e[0:1, bass.ds(2 * SLOTS * g, 2 * SLOTS)], engines=[mybir.EngineType.Activation], min_val=0, max_val=E - 1,
                    skip_runtime_bounds_check_because="tile_e is a count of 0 or more, kept to E - 1 by a minimum")[1]
                for k in range(SLOTS):
                    if k < SLOTS - 1:
                        copy_tileT(g, k + 1)
                    elif not last:
                        copy_tileT(g + 1, 0)
                    silus(g, k, experts[2 * k:2 * k + 2])

            group(0)
            with act.Fori(0, NG - 2) as gi:
                group(gi + 1)
            group(NG - 1, last=True)

        @block.tensor
        def _(pe):
            pe.wait_ge(bd_ready, 1)
            nc.tensor.transpose(PS[:, 0, 0:P], wo_sb[:], ident[:])
            nc.tensor.matmul(PS[:, 1, 0:P], wk_bd[:].rearrange("p h d -> p (h d)"),
                             wq_bd[:].rearrange("p h d -> p (h d)"), start=True, stop=True).then_inc(wo_psum, 1)
            pe.wait_ge(wo_copied, 1)
            nc.tensor.matmul(PS[:, 0, 0:P], wv_bd[:].rearrange("p h d -> p (h d)"), woT[:],
                             start=True, stop=True).then_inc(wvo_psum, 1)
            nc.tensor.transpose(PS[:, 4, 0:E], rw[:], ident[0:E, 0:E]).then_inc(rw_psum, 1)
            pe.wait_ge(rw_copied, 1)

            def prep(q, qs, part, arrived):
                if part == 0:
                    ge(pe, kp_copied, 2 * q)
                else:
                    ge(pe, prep_copied, 2 * q + part)
                if part == 0:
                    pe.wait_ge(xn_ready, q + 1)
                    for j in range(QB):
                        ins = nc.tensor.transpose(PS[:, 6, j * P:(j + 1) * P], xn[:, j, :], ident[:])
                elif part == 1:
                    pe.wait_ge(ctx_in[qs], 16 * arrived)
                    for j in range(QB):
                        ins = nc.tensor.transpose(PS[:, 6, j * SK:(j + 1) * SK],
                                                  ctxq[:, qs, j, :], ident[0:SK, 0:SK])
                else:
                    ins = nc.tensor.matmul(PS[:, 6, 0:QB * SK], MT[:], ctxT[:], start=True, stop=True)
                ins.then_inc(prep_psum, 1)

            def scores(b, j, qs, u):
                ge(pe, exp_done, 2 * (b - 1) + u + 1)
                for g in (2 * u, 2 * u + 1):
                    nc.tensor.matmul(PS[:, g, 0:GK], identb[:], maskneg[:].rearrange("p i k -> p (i k)"),
                                     start=True, stop=False)
                for n, (x, k) in enumerate(((0, 0), (1, 0), (0, 1))):
                    for g in (2 * u, 2 * u + 1):
                        r = slice(g * GR, (g + 1) * GR)
                        ins = nc.tensor.matmul(PS[:, g, 0:GK], xT[x][r, qs, j * P:(j + 1) * P],
                                               kbd[k][r, qs, j].rearrange("p i k -> p (i k)"), start=False, stop=n == 2,
                                               tile_position=(g * GR, 0))
                ins.then_inc(scores_ready, 1)

            def transpose_max(b, u, back):
                pe.wait_ge(max_ready, 2 * b + u + 1)
                ge(pe, mt_copied, 2 * b + u)
                if u == 1 and back:
                    pe.wait_ge(spread_copied, b - 1)
                nc.tensor.transpose(PS[:, 6, 0:P], nm[:, u, :], ident[:]).then_inc(mt_psum, 1)

            def shift(b, u):
                pe.wait_ge(mt_copied, 2 * b + u + 1)
                for g in (2 * u, 2 * u + 1):
                    r = slice(g * GR, (g + 1) * GR)
                    ins = nc.tensor.matmul(PS[:, g, 0:GK], mT[r, u, :], ind[r].rearrange("p i k -> p (i k)"),
                                           start=False, stop=True, tile_position=(g * GR, 0),
                                           skip_group_check=True)
                ins.then_inc(shifted, 1)

            def transpose_probs(b, s, u):
                pe.wait_ge(exp_done, 2 * b + u + 1)
                for v in range(2):
                    ge(pe, pt_copied[v], 2 * b + u)
                    for i in range(GH):
                        ins = nc.tensor.transpose(PS[0:SK, 4 + v, i * P:(i + 1) * P], prob[:, s, u, v, i, 0:SK], ident[:])
                    ins.then_inc(pt_psum[v], 1)

            def weigh(b, s, heads):
                if heads[0] == 0:
                    for v in range(2):
                        pe.wait_ge(pt_copied[v], 2 * b + 2)
                    pe.wait_ge(vm_ready, b + 1)
                    ge(pe, x1_done, b)
                for i in heads:
                    for g in range(G):
                        ins = nc.tensor.matmul(PS[g * GR:(g + 1) * GR, 7, 0:P], vm[:, s, g, i, :],
                                         PT[:, s, g, i * P:(i + 1) * P], start=i == 0, stop=i == GH - 1,
                                         tile_position=(0, g * GR))
                        if i == GH - 1 and g == G - 1:
                            ins.then_inc(pv_done, 1)

            def spread_sums(b, s, maxima):
                pe.wait_ge(rinv_done, b + 1)
                ge(pe, mt_copied, maxima)
                ge(pe, spread_copied, b)
                nc.tensor.matmul(PS[:, 6, P:2 * P], rinv[:, s].rearrange("p h d -> p (h d)"), ident[:],
                                 start=True, stop=True).then_inc(spread_psum, 1)

            def project(b):
                pe.wait_ge(o_ready, b + 1)
                nc.tensor.matmul(PS[:, 7, 2 * P:2 * P + D], oT[:], WVO[:], start=True, stop=True).then_inc(proj_done, 1)

            for part_ in range(3):
                prep(0, 0, part_, 1)

            def step_of(b, s, j, front, mid, back, q=None, q2=None, arrived=None, prepare=False, preps=0, keys=0):
                if front:
                    scores(b, j, q2, 0)
                if mid:
                    transpose_probs(b - 1, 1 - s, 0)
                if front:
                    scores(b, j, q2, 1)
                    ge(pe, prep_copied, preps)
                    ge(pe, kp_copied, keys)
                if back:
                    spread_sums(b - 2, s, 2 * min(b, B) if isinstance(b, int) else 2 * b)
                if front:
                    transpose_max(b, 0, back)
                if mid:
                    transpose_probs(b - 1, 1 - s, 1)
                if front:
                    shift(b, 0)
                if back:
                    weigh(b - 2, s, (0, 1))
                if front:
                    transpose_max(b, 1, back)
                if back:
                    weigh(b - 2, s, (2, 3))
                if front:
                    shift(b, 1)
                if prepare and j < 3:
                    pe.wait_ge(mt_copied, 2 * b + 2)
                    prep(q + 1, 1 - q2, j, arrived)
                if back:
                    project(b - 2)

            def quad(q, q2, arrived=None, last=False):
                for j in range(QB):
                    b = q * QB + j
                    pe.wait_ge(kbd_ready, b + 1)
                    at = b if isinstance(b, int) else 2
                    done = q if last else q + 1
                    preps = 2 * (q + 1) + (0 if last else min(j, 2))
                    keys = 2 * (q + 1) + (2 if j == 3 and not last else 0)
                    step_of(b, j % 2, j, True, at >= 1, at >= 2, q, q2, arrived, not last, preps, keys)

            quad(0, 0, 1)
            with pe.Fori(0, (NQ - 2) // 2) as i2:
                quad(2 * i2 + 1, 1, i2 + 2)
                quad(2 * i2 + 2, 0, i2 + 2)
            quad(NQ - 1, 1, last=True)
            step_of(B, 0, 0, False, True, True)
            step_of(B + 1, 1, 1, False, False, True)

            pe.wait_ge(pt_copied[1], 2 * B)

            def transpose_h(q, s):
                pe.wait_ge(h_ready, q + 1)
                ge(pe, hT_copied, q - 1)
                for j in range(QB):
                    ins = nc.tensor.transpose(PS[:, 5 + s, j * P:(j + 1) * P], xn2[:, s, j, :], ident[:])
                ins.then_inc(hT_psum, 1)

            def logits_of(q, s):
                pe.wait_ge(hT_copied, q + 1)
                for j in range(QB):
                    ins = nc.tensor.matmul(PS[:, 4, bass.ds(q * QB * E + j * E, E)],
                                           hq[:, s, j * P:(j + 1) * P], RWT[:], start=True, stop=True)
                ins.then_inc(logits_done, 1)

            def pair(i, last=False):
                transpose_h(2 * i + 1, 1)
                logits_of(2 * i, 0)
                if not last:
                    transpose_h(2 * i + 2, 0)
                logits_of(2 * i + 1, 1)

            transpose_h(0, 0)
            pair(0)
            with pe.Fori(0, NQ // 2 - 2) as i2:
                pair(i2 + 1)
            pair(NQ // 2 - 1, last=True)

            pe.wait_ge(eq_ready, 1)
            nc.tensor.matmul(PS[:, 0, :], trib[:], eqb[:].rearrange("p b e -> p (b e)"), start=True, stop=True)
            nc.tensor.matmul(PS[:, 1, :], onesb[:], eqb[:].rearrange("p b e -> p (b e)"),
                             start=True, stop=True).then_inc(ranks_psum, 1)

            pe.wait_ge(quantised, 1)
            for e in range(NE):
                if e >= 2:
                    pe.wait_ge(wT_copied, e - 1)
                for f in range(FB):
                    nc.tensor.transpose(PS[:, 2 * (e % 2), f * P:(f + 1) * P], w1n[:, e, f, :], ident[:])
                for f in range(FB):
                    ins = nc.tensor.transpose(PS[:, 2 * (e % 2) + 1, f * P:(f + 1) * P],
                                              w2n[:, e, f * P:(f + 1) * P], ident[:])
                ins.then_inc(wT_psum, 1)

            def load_experts(first_tile, n):
                return nc.values_load_multi_w_load_instructions(
                    tile_e[0:1, bass.ds(first_tile, n)], engines=[mybir.EngineType.PE], min_val=0, max_val=E - 1,
                    skip_runtime_bounds_check_because="tile_e is a count of 0 or more, kept to E - 1 by a minimum")[1]

            def transpose_tile(g, k):
                n = g * SLOTS + k
                pe.wait_ge(xh_ready, n + 1)
                ge(pe, tileT_copied, n)
                for a in range(2):
                    ins = nc.tensor.transpose(PS[:, 6, a * P:(a + 1) * P], xh[:, k % 2, a], ident[:])
                ins.then_inc(tileT_psum, 1)

            def first_layer(g, k, experts):
                n = g * SLOTS + k
                s = k % 2
                pe.wait_ge(split_done, n + 1)
                ge(pe, silu_done, n - 1)
                for f in range(FB):
                    for h in range(3):
                        ins = nc.tensor.matmul(PS[:, s, f * 2 * P:(f + 1) * 2 * P], W1T[:, E, f, :], hpart[:, s, h],
                                               start=h == 0, stop=h == 2)
                ins.then_inc(zs_psum, 1)
                for a in range(2):
                    e = experts[a]
                    for f in range(FB):
                        for h in range(3):
                            ins = nc.tensor.matmul(PS[:, 2 + s, (2 * a + f) * P:(2 * a + f + 1) * P],
                                                   W1T[:, bass.ds(e, 1), f, :].squeeze(1), hpart[:, s, h, a * P:(a + 1) * P],
                                                   start=h == 0, stop=h == 2)
                ins.then_inc(zr_psum, 1)

            def second_layer(g, k, experts):
                n = g * SLOTS + k
                s = k % 2
                pe.wait_ge(silu_done, n + 1)
                ge(pe, res_ready, n - 1)
                for a in range(2):
                    for f in range(FB):
                        nc.tensor.matmul(PS[:, 4 + s, 2 * a * P:(2 * a + 1) * P], h1s[:, s, f, a * P:(a + 1) * P],
                                         W2T[:, E, f, :], start=f == 0, stop=f == FB - 1)
                    e = experts[a]
                    for f in range(FB):
                        ins = nc.tensor.matmul(PS[:, 4 + s, (2 * a + 1) * P:(2 * a + 2) * P], h1r[:, s, a, f],
                                               W2T[:, bass.ds(e, 1), f, :].squeeze(1), start=f == 0, stop=f == FB - 1)
                ins.then_inc(y_psum, 1)

            pe.wait_ge(tables_ready, 1)
            pe.wait_ge(wT_copied, NE)
            transpose_tile(0, 0)

            def group(g, first=False, last=False):
                experts = load_experts(0, 2 * SLOTS) if first else load_experts(2 * SLOTS * g - 4, 2 * SLOTS + 4)
                if not first:
                    before, experts = experts[2:4], experts[4:]
                for k in range(SLOTS):
                    if k < SLOTS - 1:
                        transpose_tile(g, k + 1)
                    elif not last:
                        transpose_tile(g + 1, 0)
                    first_layer(g, k, experts[2 * k:2 * k + 2])
                    if k > 0:
                        second_layer(g, k - 1, experts[2 * k - 2:2 * k])
                    elif not first:
                        second_layer(g - 1, SLOTS - 1, before)
                return experts[2 * SLOTS - 2:]

            group(0, first=True)
            with pe.Fori(0, NG - 2) as gi:
                group(gi + 1)
            second_layer(NG - 1, SLOTS - 1, group(NG - 1, last=True))


NAMES = {"x": "x", "ctx": "ctx_1024", "mask": "mask_1x1xSxS2_ik0", "g_x": "g_xattn", "g_f": "g_ffn",
         "Wq": "L0_xattn_Wq", "Wk": "L0_xattn_Wk", "Wv": "L0_xattn_Wv", "Wo": "L0_xattn_Wo", "bo": "L0_xattn_bo",
         "sw1": "L0_ffn_shared_w1", "sw2": "L0_ffn_shared_w2", "ew1": "L0_ffn_expert_w1",
         "ew2": "L0_ffn_expert_w2", "rw": "L0_ffn_router_w", "gamma": "L0_ffn_ln_gamma", "beta": "L0_ffn_ln_beta"}


def kernel(**inputs):
    import concourse.bacc as bacc
    from concourse.bass_utils import run_bass_kernel_spmd

    nc = bacc.Bacc("TRN2", target_bir_lowering=False, num_devices=1)
    arrays, args = {}, {}
    for short, name in NAMES.items():
        a = np.ascontiguousarray(inputs[name])
        arrays[f"in_{short}"] = a
        args[short] = nc.dram_tensor(f"in_{short}", a.shape, mybir.dt.from_np(a.dtype), kind="ExternalInput").ap()
    args["out"] = nc.dram_tensor("out", (B, SQ, D), FP32, kind="ExternalOutput").ap()
    args["rows"] = nc.dram_tensor("rows", (E * REGION + P, ROW), FP32, kind="Internal").ap()
    build(nc, args)
    r = run_bass_kernel_spmd(nc, [arrays], core_ids=[0])
    return r.results[0]["out"]
```

```python
import numpy as np
import concourse.bass as bass
from concourse import mybir
from contextlib import ExitStack

FP32 = mybir.dt.float32
BF16 = mybir.dt.bfloat16
I32 = mybir.dt.int32
FP32R = mybir.dt.float32r
ALU = mybir.AluOpType
ACT = mybir.ActivationFunctionType
AX = mybir.AxisListType

P = 128
B, SQ, D = 64, 128, 128
SK = 77
H = 16
HD = D // H
GH = 4
G = H // GH
GR = P // G
GK = GH * SK
SP = SK + 1
RN = SP // 6
QB = 4
NQ = B // QB
XC = 8
E, F = 8, 256
FB = F // P
NE = E + 1
EPS = 1e-5
TOKENS = B * SQ
REGION = TOKENS + P
ROW = D + 4
NT = -(-(TOKENS // P + E - 1) // 12) * 12
LG = 384
PAYS = 4
SLOTS = 6
NG = NT // 2 // SLOTS
MASKED = -1e20
BANK = 512


def ge(eng, sem, value):
    if not isinstance(value, int) or value > 0:
        eng.wait_ge(sem, value)


def build(nc, A):
    ctx = ExitStack()
    with ctx:
        def sb(name, shape, dt=FP32):
            return ctx.enter_context(nc.sbuf_tensor(name, shape, dt))

        def sem(name):
            return ctx.enter_context(nc.semaphore(name))

        PS = ctx.enter_context(nc.psum_tensor("PS", [P, 8, BANK], FP32))

        X = sb("X", [P, B, D])
        ctxq = sb("ctxq", [SK, 2, QB, D])
        ident = sb("ident", [P, P])
        identb = sb("identb", [P, P], BF16)
        ones = sb("ones", [P, P])
        headsel = sb("headsel", [P, H, HD])
        rowsel = sb("rowsel", [P, GH])
        shiftsel = sb("shiftsel", [P, GH])
        ind = sb("ind", [P, GH, SK], FP32R)
        mask_i = sb("mask_i", [P, SK], I32)
        maskneg = sb("maskneg", [P, GH, SK], BF16)
        wq8 = sb("wq8", [P, HD])
        wk8 = sb("wk8", [P, HD])
        wv8 = sb("wv8", [P, HD])
        wq_bd = sb("wq_bd", [P, H, HD])
        wk_bd = sb("wk_bd", [P, H, HD])
        wv_bd = sb("wv_bd", [P, H, HD])
        wo_sb = sb("wo_sb", [P, D])
        woT = sb("woT", [P, D])
        MT = sb("MT", [P, P])
        WVO = sb("WVO", [P, D])
        gx = sb("gx", [P, 1])
        gf = sb("gf", [P, 1])
        tgx = sb("tgx", [P, 1])
        tgf = sb("tgf", [P, 1])
        bo = sb("bo", [P, D])
        gamma = sb("gamma", [P, 1])
        beta = sb("beta", [P, 1])
        w1n = sb("w1n", [P, NE, FB, D])
        w2n = sb("w2n", [P, NE, F])
        wabs = sb("wabs", [P, NE, FB])
        half = sb("half", [P, NE, FB])
        nhalf = sb("nhalf", [P, NE, FB])
        wabs2 = sb("wabs2", [P, NE])
        half2 = sb("half2", [P, NE])
        nhalf2 = sb("nhalf2", [P, NE])
        work = sb("work", [P, NE * F])
        neg1 = work[:].rearrange("p (e b d) -> p e b d", e=NE, b=FB)
        W1T = sb("W1T", [P, NE, FB, P], BF16)
        W2T = sb("W2T", [P, NE, FB, P])
        rw = sb("rw", [E, D])
        carrier = sb("carrier", [P, 1])
        dve_carrier = sb("dve_carrier", [P, 1])
        act_carrier = sb("act_carrier", [P, 1])
        spare = sb("spare", [P, QB])
        RWT = sb("RWT", [P, E])
        st = sb("st", [P, B, 6])
        mv = sb("mv", [P, B, 2])
        ve = sb("ve", [P, B])
        sd = sb("sd", [P, B])
        rstd = sb("rstd", [P, B])
        nmr = sb("nmr", [P, B])
        xn = sb("xn", [P, QB, D])
        xT = [sb(f"xT_{w}", [P, 2, QB * P], FP32R) for w in ("hi", "lo")]
        ctxT = sb("ctxT", [P, QB * SK])
        kp = [sb(f"kp_{w}", [P, QB * SK]) for w in ("hi", "lo")]
        kbd = [sb(f"kbd_{w}", [P, 2, QB, GH, SK], FP32R) for w in ("hi", "lo")]
        vm = sb("vm", [SK, 2, G, GH, GR])
        mx = sb("mx", [P, 2, 2, GH])
        nm = sb("nm", [P, 2, P])
        mT = sb("mT", [P, 2, P], FP32R)
        prob = sb("prob", [P, 2, 2, 2, GH, SP])
        part = sb("part", [P, H, SP // 2])
        shared = sb("shared", [P, 2 * H * P])
        PT = shared[0:SK, :].rearrange("p (s g c) -> p s g c", s=2, g=G)
        rsum = sb("rsum", [P, 2, H])
        rrec = sb("rrec", [P, H])
        rinv = sb("rinv", [P, 2, H, HD])
        rspread = sb("rspread", [P, P])
        oT = sb("oT", [P, P])
        lg = sb("lg", [P, B, E])
        lmax = sb("lmax", [P, B])
        eq = sb("eq", [P, B, E])
        rank = sb("rank", [P, E])
        best = sb("best", [P, B])
        gate = sb("gate", [P, B, E])
        topp = sb("topp", [P, B])
        hq = sb("hq", [P, BANK])
        stq = sb("stq", [P, QB, 6])
        mvq = sb("mvq", [P, QB, 2])
        veq = sb("veq", [P, QB])
        invq = sb("invq", [P, QB])
        rsq = sb("rsq", [P, QB])
        nmq = sb("nmq", [P, QB])
        mhalf = sb("mhalf", [P, QB])
        threehalf = sb("threehalf", [P, QB])
        minus = sb("minus", [P, QB])
        sdq = sb("sdq", [P, QB])
        trib = sb("trib", [P, P], BF16)
        onesb = sb("onesb", [P, P], BF16)
        eqb = sb("eqb", [P, B, E], BF16)
        region0 = sb("region0", [P, NE])
        num = sb("num", [P, NT])
        num_i = sb("num_i", [P, NT], I32)
        tok_i = sb("tok_i", [P, B], I32)
        scan = sb("scan", [P, 2, B // 2, E])
        free_row = sb("free_row", [P, 3, E])
        counts = sb("counts", [P, E])
        pos = sb("pos", [P, B])
        pos_i = sb("pos_i", [P, B], I32)
        tiles_of = sb("tiles_of", [P, 3, E])
        gap = sb("gap", [P, E])
        cmp_k = sb("cmp_k", [P, E, TOKENS // P])
        cmp_t = sb("cmp_t", [P, NT, E])
        tile_f = sb("tile_f", [P, NT])
        tile_e = sb("tile_e", [P, NT], I32)
        tile_row = sb("tile_row", [P, NT], I32)
        pad_row_i = sb("pad_row_i", [P, NE], I32)
        padding = sb("padding", [P, ROW])
        pay = prob[:].rearrange("p a b c d e -> p (a b c d e)")[:, 0:PAYS * QB * ROW].rearrange("p (s b r) -> p s b r", s=PAYS, b=QB)
        pay_i = sb("pay_i", [P, PAYS, QB], I32)
        tin = sb("tin", [P, SLOTS, 2, ROW])
        xh = sb("xh", [P, 2, 2, D])
        hT = sb("hT", [P, 2, 2 * P])
        rest = sb("rest", [P, 2 * P])
        hpart = sb("hpart", [P, 2, 3, 2 * P], BF16)
        h1s = shared[:, 0:4 * F].rearrange("p (s f c) -> p s f c", s=2, f=FB)
        h1r = shared[:, 4 * F:8 * F].rearrange("p (s a f c) -> p s a f c", s=2, a=2, f=FB)
        res = sb("res", [P, SLOTS, 2, D])

        x_in = [sem(f"x_in{c}") for c in range(XC)]
        w_in, ffw_in = sem("w_in"), sem("ffw_in")
        ctx_in = [sem("ctx_in0"), sem("ctx_in1")]
        pool_c, dve_c = sem("pool_step"), sem("dve_step")
        consts_ready, var_ready, sd_ready, stats_ready = (sem(x) for x in ("consts_ready", "var_ready", "sd_ready", "stats_ready"))
        tanh_ready, bd_ready, wo_psum, wo_copied = (sem(x) for x in ("tanh_ready", "bd_ready", "wo_psum", "wo_copied"))
        wvo_psum, quantised, wT_psum, wT_copied = (sem(x) for x in ("wvo_psum", "quantised", "wT_psum", "wT_copied"))
        xb_ready, top_ready, gexp_ready = (sem(x) for x in ("xb_ready", "top_ready", "gexp_ready"))
        xn_ready, vm_ready = sem("xn_ready"), sem("vm_ready")
        prep_psum, prep_copied = sem("prep_psum"), sem("prep_copied")
        scores_ready, max_ready = sem("scores_ready"), sem("max_ready")
        mt_psum, mt_copied = sem("mt_psum"), sem("mt_copied")
        shifted, exp_done = sem("shifted"), sem("exp_done")
        pt_psum = [sem("pt_psum0"), sem("pt_psum1")]
        pt_copied = [sem("pt_copied0"), sem("pt_copied1")]
        pv_done, o_ready, proj_done, x1_done = sem("pv_done"), sem("o_ready"), sem("proj_done"), sem("x1_done")
        spread_psum, spread_copied = sem("spread_psum"), sem("spread_copied")
        x1_stats, kp_copied, kbd_ready = sem("x1_stats"), sem("kp_copied"), sem("kbd_ready")
        mx_done, hi_done, part_step, part_done = sem("mx_done"), sem("hi_done"), sem("part_step"), sem("part_done")
        rsum_done, rinv_done, xhi_done = (sem(x) for x in ("rsum_done", "rinv_done", "xhi_done"))
        h_ready, hT_psum, hT_copied, logits_done = sem("h_ready"), sem("hT_psum"), sem("hT_copied"), sem("logits_done")
        norm_step, logits_kept = sem("norm_step"), sem("logits_kept")
        root_step = sem("root_step")
        eq_ready, ranks_psum, pos_ready, tables_ready = (sem(x) for x in ("eq_ready", "ranks_psum", "pos_ready", "tables_ready"))
        pay_ready = sem("pay_ready")
        rw_psum, rw_copied = sem("rw_psum"), sem("rw_copied")
        sorted_out = [sem(f"sorted_out{k}") for k in range(PAYS)]
        pads_out, carried, act_carried = sem("pads_out"), sem("carried"), sem("act_carried")
        tile_in = [sem(f"tile_in{k}") for k in range(SLOTS)]
        xh_ready, tileT_psum, tileT_copied, h_part, split_done = (sem(x) for x in ("xh_ready", "tileT_psum", "tileT_copied", "h_part", "split_done"))
        zs_psum, zr_psum, silu_done, y_psum, y_sum, res_ready = (sem(x) for x in ("zs_psum", "zr_psum", "silu_done", "y_psum", "y_sum", "res_ready"))
        rrec_done = sem("rrec_done")
        out_done = [sem(f"out_done{k}") for k in range(SLOTS)]

        block = ctx.enter_context(nc.Block())
        N_W = 8 + 3

        @block.sync
        def _(sp):
            for c in range(XC):
                n = B // XC
                sp.dma_start(X[:, c * n:(c + 1) * n, :],
                             A["x"][c * n:(c + 1) * n].rearrange("b q d -> q b d")).then_inc(x_in[c], 16)

            def load_ctx(q, s):
                ge(sp, vm_ready, QB * (q - 1))
                ge(sp, prep_psum, 3 * (q - 2) + 2)
                sp.dma_start(ctxq[:, s], A["ctx"][bass.ds(q * QB, QB)].rearrange("b k d -> k b d")).then_inc(ctx_in[s], 16)

            load_ctx(0, 0)
            load_ctx(1, 1)
            with sp.Fori(0, (NQ - 2) // 2) as i2:
                load_ctx(2 * i2 + 2, 0)
                load_ctx(2 * i2 + 3, 1)
            sp.wait_ge(tables_ready, 1)
            for e in range(NE):
                row = sp.value_load(pad_row_i[0:1, e:e + 1], min_val=0, max_val=E * REGION)
                sp.dma_start(A["rows"][bass.ds(row, P), :], padding[:]).then_inc(pads_out, 16)

            for k in range(PAYS):
                sp.wait_ge(sorted_out[k], 16 * B // PAYS)
            sp.wait_ge(pads_out, 16 * NE)

            def group(g, first=False):
                for k in range(SLOTS):
                    if not first:
                        sp.wait_ge(out_done[k], 32 * g)
                    for a in range(2):
                        row = sp.value_load(tile_row[0:1, bass.ds((g * SLOTS + k) * 2 + a, 1)], min_val=0, max_val=E * REGION)
                        sp.dma_start(tin[:, k, a, :], A["rows"][bass.ds(row, P), :]).then_inc(tile_in[k], 16)

            group(0, True)
            with sp.Fori(0, NG - 1) as gi:
                group(gi + 1)
            for k in range(SLOTS):
                sp.wait_ge(out_done[k], 32 * NG)

        @block.gpsimd
        def _(pool):
            n = [0]

            def step(ins):
                n[0] += 1
                ins.then_inc(pool_c, 1)
                pool.wait_ge(pool_c, n[0])

            def band(t, pattern, base_lo, base_hi, cm):
                step(nc.gpsimd.affine_select(out=t, in_=t, compare_op=ALU.is_ge, fill=0.0, base=base_lo,
                                             pattern=pattern, channel_multiplier=cm))
                step(nc.gpsimd.affine_select(out=t, in_=t, compare_op=ALU.is_ge, fill=0.0, base=base_hi,
                                             pattern=[[-s, c] for s, c in pattern], channel_multiplier=-cm))

            step(nc.gpsimd.memset(ident[:], 0.0))
            step(nc.gpsimd.affine_select(out=ident[:], in_=ident[:], compare_op=ALU.not_equal, fill=1.0,
                                         base=0, pattern=[[-1, P]], channel_multiplier=1))
            step(nc.gpsimd.memset(headsel[:], 1.0))
            band(headsel[:], [[-HD, H], [0, HD]], 0, HD - 1, 1)
            step(nc.gpsimd.memset(vm[:], 0.0))
            step(nc.gpsimd.memset(ones[:], 1.0))
            for t, value in ((mhalf, -0.5), (threehalf, 1.5), (minus, -1.0)):
                step(nc.gpsimd.memset(t[:], value))
            step(nc.gpsimd.memset(nm[:], 0.0))
            step(nc.gpsimd.memset(prob[:], 0.0))
            for i in range(E):
                step(nc.gpsimd.memset(rank[:, i:i + 1], float(E - i)))
            step(nc.gpsimd.tensor_tensor(rowsel[:], headsel[:, 0:GH, 0], headsel[:, GH:2 * GH, 0], ALU.add))
            for g in range(2, G):
                step(nc.gpsimd.tensor_tensor(rowsel[:], rowsel[:], headsel[:, g * GH:(g + 1) * GH, 0], ALU.add))
            step(nc.gpsimd.tensor_tensor(shiftsel[:], ident[:, 0:GH], ident[:, GR:GR + GH], ALU.add))
            for g in range(2, G):
                step(nc.gpsimd.tensor_tensor(shiftsel[:], shiftsel[:], ident[:, g * GR:g * GR + GH], ALU.add))
            for g in range(G):
                step(nc.gpsimd.tensor_tensor(shiftsel[:], shiftsel[:], ident[:, g * GR + GH:g * GR + 2 * GH], ALU.add))
            step(nc.gpsimd.tensor_copy(ind[:], shiftsel[:].unsqueeze(2).broadcast_to([P, GH, SK])))
            step(nc.gpsimd.tensor_copy(identb[:], ident[:]))
            step(nc.gpsimd.memset(onesb[:], 1.0))
            step(nc.gpsimd.affine_select(out=trib[:], in_=onesb[:], compare_op=ALU.is_ge, fill=0.0, base=-1,
                                         pattern=[[1, P]], channel_multiplier=-1))
            for i in range(NE):
                step(nc.gpsimd.memset(region0[:, i:i + 1], float(i * REGION)))
            step(nc.gpsimd.iota(num_i[:], pattern=[[1, NT]], base=0, channel_multiplier=0))
            step(nc.gpsimd.tensor_copy(num[:], num_i[:]))
            step(nc.gpsimd.iota(tok_i[:], pattern=[[SQ, B]], base=0, channel_multiplier=1))
            step(nc.gpsimd.memset(padding[:], 0.0))
            step(nc.gpsimd.memset(padding[:, ROW - 1:ROW].bitcast(I32), TOKENS))
            pool.sem_inc(consts_ready, 1)

            pool.wait_ge(bd_ready, 1)

            def own_columns(v):
                return bass.AP(v.tensor, v.offset, [list(v.ap[0]), [GH * GR, G], [GR + HD, GH], [1, HD]])

            def make_vm(b, j, s):
                ge(pool, pv_done, b - 1)
                nc.gpsimd.tensor_tensor(own_columns(vm[:, j % 2]),
                                        ctxq[:, s, j, :].rearrange("k (g i c) -> k g i c", g=G, i=GH),
                                        ones[0:SK, 0:P].rearrange("k (g i c) -> k g i c", g=G, i=GH),
                                        ALU.mult).then_inc(vm_ready, 1)
                xb = X[:, bass.ds(b, 1), :].squeeze(1)
                nc.gpsimd.tensor_tensor(xb, xb, bo[:], ALU.add).then_inc(xb_ready, 1)

            def expand_keys(b, q, s, j):
                pool.wait_ge(kp_copied, 2 * (q + 1))
                for w in range(2):
                    ins = nc.gpsimd.tensor_tensor(
                        kbd[w][:, s, j], kp[w][:, j * SK:(j + 1) * SK].unsqueeze(1).broadcast_to([P, GH, SK]),
                        rowsel[:].unsqueeze(2).broadcast_to([P, GH, SK]), ALU.mult)
                ins.then_inc(kbd_ready, 1)

            def add_probs(b, s):
                pool.wait_ge(exp_done, 2 * b + 2)
                ge(pool, rsum_done, b)
                p = prob[:, s].rearrange("p u v i k -> p (u v i) k")
                m = SP // 2
                nc.gpsimd.tensor_tensor(part[:], p[:, :, 0:m], p[:, :, m:SP], ALU.add).then_inc(part_step, 1)
                pool.wait_ge(part_step, 2 * b + 1)
                nc.gpsimd.tensor_tensor(part[:, :, 0:RN], part[:, :, 0:RN], part[:, :, RN:2 * RN], ALU.add).then_inc(part_step, 1)
                pool.wait_ge(part_step, 2 * b + 2)
                nc.gpsimd.tensor_tensor(part[:, :, 0:RN], part[:, :, 0:RN], part[:, :, 2 * RN:3 * RN], ALU.add).then_inc(part_done, 1)

            def root(q):
                ge(pool, root_step, 11 * q)
                ge(pool, h_ready, q)
                pool.wait_ge(norm_step, 3 * q + 3)
                for k, (to, in0, in1, op) in enumerate((
                        (invq, veq, mhalf, ALU.pow), (sdq, invq, invq, ALU.mult), (sdq, sdq, veq, ALU.mult),
                        (sdq, sdq, mhalf, ALU.mult), (sdq, sdq, threehalf, ALU.add), (rsq, invq, sdq, ALU.mult),
                        (nmq, mvq, rsq, ALU.mult), (nmq, nmq, minus, ALU.mult))):
                    nc.gpsimd.tensor_tensor(to[:], in0[:, :, 0] if in0 is mvq else in0[:], in1[:], op).then_inc(root_step, 1)
                    pool.wait_ge(root_step, 11 * q + k + 1)

            def keep_root(q):
                quad_ = slice(q * QB, (q + 1) * QB) if isinstance(q, int) else bass.ds(q * QB, QB)
                nc.gpsimd.tensor_copy(rstd[:, quad_], rsq[:]).then_inc(root_step, 1)
                nc.gpsimd.tensor_copy(nmr[:, quad_], nmq[:]).then_inc(root_step, 1)

            def quad(q, s, arrived, last=False):
                pool.wait_ge(xn_ready, q + 1)
                pool.wait_ge(ctx_in[s], 16 * arrived)
                for j in range(QB):
                    b = q * QB + j
                    if not (isinstance(b, int) and b == 0):
                        add_probs(b - 1, (j - 1) % 2)
                    if j == 2 and not (isinstance(q, int) and q == 0):
                        root(q - 1)
                    if j < QB - 1:
                        expand_keys(b + 1, q, s, j + 1)
                    elif not last:
                        expand_keys(b + 1, q + 1, 1 - s, 0)
                    make_vm(b, j, s)
                    if j == 2 and not (isinstance(q, int) and q == 0):
                        nc.gpsimd.tensor_tensor(spare[:], mhalf[:], mhalf[:], ALU.add).then_inc(root_step, 1)
                        keep_root(q - 1)

            expand_keys(0, 0, 0, 0)

            for q in range(3):
                quad(q, q % 2, q // 2 + 1)
            with pool.Fori(0, (NQ - 4) // 2) as i2:
                quad(2 * i2 + 3, 1, i2 + 2)
                quad(2 * i2 + 4, 0, i2 + 3)
            quad(NQ - 1, 1, NQ // 2, last=True)
            add_probs(B - 1, 1)
            root(NQ - 1)
            nc.gpsimd.tensor_tensor(spare[:], mhalf[:], mhalf[:], ALU.add).then_inc(root_step, 1)
            keep_root(NQ - 1)

            def carry(n):
                pool.wait_ge(carried, n + 1)
                nc.gpsimd.tensor_tensor(carrier[:], rank[:, 0:1], rank[:, 0:1], ALU.add).then_inc(carried, 1)

            nc.gpsimd.memset(carrier[:], 0.0).then_inc(carried, 1)
            def row_of(idx):
                return bass.IndirectOffsetOnAxis(ap=idx.bitcast(mybir.dt.uint32), axis=0)

            def sort_quad(q, s):
                pool.wait_ge(pay_ready, q + 1)
                carry(q)
                for j in range(QB):
                    nc.gpsimd.indirect_dma_start(out=A["rows"][:, :], out_offset=row_of(pay_i[:, s, j:j + 1]),
                                                 in_=pay[:, s, j, :], in_offset=None).then_inc(sorted_out[s], 16)

            with pool.Fori(0, NQ // PAYS) as i4:
                for s in range(PAYS):
                    sort_quad(PAYS * i4 + s, s)
            def group(g):
                for k in range(SLOTS):
                    pool.wait_ge(res_ready, g * SLOTS + k + 1)
                    carry(NQ + g * SLOTS + k)
                    for a in range(2):
                        nc.gpsimd.indirect_dma_start(out=A["out"].rearrange("b q d -> (b q) d"),
                                                     out_offset=row_of(tin[:, k, a, ROW - 1:ROW]),
                                                     in_=res[:, k, a, :], in_offset=None,
                                                     bounds_check=TOKENS - 1, oob_is_err=False).then_inc(out_done[k], 16)

            with pool.Fori(0, NG) as gi:
                group(gi)

        @block.vector
        def _(dve):
            n = [0]

            def step(ins, signal=None):
                if signal is not None:
                    ins.then_inc(signal, 1)
                    dve.wait_ge(signal, 1)
                    return
                n[0] += 1
                ins.then_inc(dve_c, 1)
                dve.wait_ge(dve_c, n[0])

            def newton(v, inv):
                step(nc.vector.tensor_tensor(sd[:], inv, inv, ALU.mult))
                step(nc.vector.tensor_tensor(sd[:], sd[:], v, ALU.mult))
                step(nc.vector.tensor_scalar(sd[:], sd[:], -0.5, 1.5, ALU.mult, ALU.add))
                step(nc.vector.tensor_tensor(inv, inv, sd[:], ALU.mult))

            for b in range(B):
                if b % (B // XC) == 0:
                    dve.wait_ge(x_in[b // (B // XC)], 16)
                ins = nc.vector.bn_stats(st[:, b, :], X[:, b, :])
            step(ins)

            dve.wait_ge(w_in, 16 * N_W)
            dve.wait_ge(consts_ready, 1)
            for bd, w in ((wq_bd, wq8), (wk_bd, wk8), (wv_bd, wv8)):
                ins = nc.vector.tensor_tensor(bd[:], w[:].unsqueeze(1).broadcast_to([P, H, HD]), headsel[:], ALU.mult)
            step(ins)
            dve.wait_ge(tanh_ready, 1)
            step(nc.vector.tensor_scalar(bo[:], bo[:], tgx[:], None, ALU.mult), bd_ready)
            for b in range(B):
                ins = nc.vector.bn_aggr(mv[:, b, :], st[:, b, :])
            step(ins)
            step(nc.vector.tensor_scalar(ve[:], mv[:, :, 1], EPS, None, ALU.add), var_ready)
            dve.wait_ge(wo_psum, 1)
            step(nc.vector.tensor_copy(woT[:], PS[:, 0, 0:P]))
            step(nc.vector.tensor_copy(MT[:], PS[:, 1, 0:P]), wo_copied)
            dve.wait_ge(sd_ready, 1)
            step(nc.vector.reciprocal(rstd[:], sd[:]))
            newton(ve[:], rstd[:])
            step(nc.vector.scalar_tensor_tensor(nmr[:], mv[:, :, 0], -1.0, rstd[:], ALU.mult, ALU.mult), stats_ready)
            step(nc.vector.tensor_scalar(maskneg[:], mask_i[:].unsqueeze(1).broadcast_to([P, GH, SK]), 0.0, MASKED,
                                         ALU.is_equal, ALU.mult))
            dve.wait_ge(wvo_psum, 1)
            step(nc.vector.tensor_scalar(WVO[:], PS[:, 0, 0:D], tgx[:], None, ALU.mult))
            dve.wait_ge(rw_psum, 1)
            step(nc.vector.tensor_copy(RWT[:], PS[:, 4, 0:E]), rw_copied)

            def prep_x(q, qs):
                dve.wait_ge(xhi_done, q + 1)
                nc.vector.tensor_tensor(xT[1][:, qs], PS[:, 6, :], xT[0][:, qs].bitcast(FP32), ALU.subtract).then_inc(prep_copied, 1)

            def prep_k(q):
                dve.wait_ge(kp_copied, 2 * q + 1)
                nc.vector.tensor_tensor(kp[1][:], PS[:, 6, 0:QB * SK], kp[0][:], ALU.subtract).then_inc(kp_copied, 1)

            def take_max(b, u):
                dve.wait_ge(scores_ready, 2 * b + u + 1)
                nc.vector.tensor_reduce(mx[:, u], PS[:, 2 * u:2 * u + 2, 0:GK].rearrange("p g (i k) -> p g i k", k=SK),
                                        AX.X, ALU.max, negate=True).then_inc(mx_done, 1)
                ge(dve, mt_psum, 2 * (b - 1) + u + 1)
                dve.wait_ge(mx_done, 2 * b + u + 1)
                cols = nm[:, u, :].rearrange("p (g r) -> p g r", g=G)[:, 2 * u:2 * u + 2]
                nc.vector.tensor_copy(cols[:, :, 0:GH].bitcast(FP32R), mx[:, u]).then_inc(hi_done, 1)
                dve.wait_ge(hi_done, 2 * b + u + 1)
                nc.vector.tensor_tensor(cols[:, :, GH:2 * GH], mx[:, u], cols[:, :, 0:GH], ALU.subtract).then_inc(max_ready, 1)

            def copy_pt(b, s, u):
                dve.wait_ge(pt_psum[1], 2 * b + u + 1)
                ge(dve, pv_done, b - 1)
                nc.vector.tensor_copy(PT[:, s, 2 * u + 1, :], PS[0:SK, 5, :]).then_inc(pt_copied[1], 1)

            def sums(b, s):
                dve.wait_ge(part_done, b + 1)
                nc.vector.tensor_reduce(rsum[:, s], part[:, :, 0:RN], AX.X, ALU.add).then_inc(rsum_done, 1)
                dve.wait_ge(rsum_done, b + 1)
                nc.vector.reciprocal(rrec[:], rsum[:, s]).then_inc(rrec_done, 1)
                dve.wait_ge(rrec_done, b + 1)
                nc.vector.tensor_copy(rinv[:, s], rrec[:].unsqueeze(2).broadcast_to([P, H, HD])).then_inc(rinv_done, 1)

            def normalise(b):
                dve.wait_ge(pv_done, b + 1)
                dve.wait_ge(spread_copied, b + 1)
                nc.vector.tensor_tensor(oT[:], PS[:, 7, 0:P], rspread[:], ALU.mult).then_inc(o_ready, 1)

            def residual(b, j):
                dve.wait_ge(proj_done, b + 1)
                dve.wait_ge(xb_ready, b + 1)
                xb = X[:, bass.ds(b, 1), :].squeeze(1)
                nc.vector.tensor_tensor(xb, xb, PS[:, 7, 2 * P:3 * P], ALU.add).then_inc(x1_done, 1)
                dve.wait_ge(x1_done, b + 1)
                nc.vector.bn_stats(st[:, bass.ds(b, 1), :].squeeze(1), xb).then_inc(x1_stats, 1)

            def then(ins, count):
                ins.then_inc(norm_step, 1)
                dve.wait_ge(norm_step, count)

            def statistics(q):
                quad_ = slice(q * QB, (q + 1) * QB) if isinstance(q, int) else bass.ds(q * QB, QB)
                dve.wait_ge(x1_stats, QB * (q + 1))
                nc.vector.tensor_scalar(stq[:], st[:, quad_, :], 1.0, None, ALU.mult).then_inc(norm_step, 1)
                dve.wait_ge(norm_step, 3 * q + 1)
                nc.vector.tensor_scalar(dve_carrier[:], stq[:, 0, 0:1], 1.0, None, ALU.mult)
                for j in range(QB):
                    ins = nc.vector.bn_aggr(mvq[:, j, :], stq[:, j, :])
                then(ins, 3 * q + 2)
                then(nc.vector.tensor_scalar(veq[:], mvq[:, :, 1], 1.0 + EPS, EPS * EPS, ALU.mult, ALU.add), 3 * q + 3)

            def keep_logits(q):
                quad_ = slice(q * QB, (q + 1) * QB) if isinstance(q, int) else bass.ds(q * QB, QB)
                nc.vector.tensor_copy(lg[:, quad_, :], PS[:, 7, LG:LG + QB * E].rearrange("p (b e) -> p b e", e=E)).then_inc(logits_kept, 1)

            prep_x(0, 0)
            prep_k(0)

            def step_of(b, s, j, front, mid, back, q=None, q2=None, prep=False, stats_of=None, logits_of=None):
                if front:
                    take_max(b, 0)
                if mid:
                    copy_pt(b - 1, 1 - s, 0)
                if front:
                    take_max(b, 1)
                if mid:
                    copy_pt(b - 1, 1 - s, 1)
                if back:
                    normalise(b - 2)
                if mid:
                    sums(b - 1, 1 - s)
                if prep and j == 0:
                    prep_x(q + 1, 1 - q2)
                if prep and j == 2:
                    prep_k(q + 1)
                if back and j == 0 and logits_of is not None:
                    dve.wait_ge(proj_done, b - 1)
                    keep_logits(logits_of)
                if back:
                    residual(b - 2, (j + 2) % QB)
                if j == 1 and stats_of is not None:
                    statistics(stats_of)

            def quad(q, q2, last=False):
                for j in range(QB):
                    b = q * QB + j
                    at = b if isinstance(b, int) else 2
                    nth = q if isinstance(q, int) else 2
                    step_of(b, j % 2, j, True, at >= 1, at >= 2, q, q2, not last,
                            stats_of=q - 1 if nth >= 1 else None, logits_of=q - 2 if nth >= 2 else None)

            for q in range(3):
                quad(q, q % 2)
            with dve.Fori(0, (NQ - 4) // 2) as i2:
                quad(2 * i2 + 3, 1)
                quad(2 * i2 + 4, 0)
            quad(NQ - 1, 1, last=True)
            step_of(B, 0, 0, False, True, True, logits_of=NQ - 2)
            step_of(B + 1, 1, 1, False, False, True, stats_of=NQ - 1)

            def route(part_):
                lo = part_ * B // 2
                half_ = slice(lo, lo + B // 2)
                shape = [P, B // 2, E]
                l, q_ = lg[:, half_], eq[:, half_]
                step(nc.vector.tensor_reduce(lmax[:, half_], l, AX.X, ALU.max))
                step(nc.vector.tensor_tensor(l, l, lmax[:, half_].unsqueeze(2).broadcast_to(shape), ALU.subtract))
                step(nc.vector.tensor_scalar(q_, l, 0.0, None, ALU.is_equal))
                step(nc.vector.tensor_tensor(q_, q_, rank[:].unsqueeze(1).broadcast_to(shape), ALU.mult))
                step(nc.vector.tensor_reduce(best[:, half_], q_, AX.X, ALU.max))
                nc.vector.tensor_tensor(q_, q_, best[:, half_].unsqueeze(2).broadcast_to(shape), ALU.is_equal).then_inc(top_ready, 1)
                dve.wait_ge(top_ready, part_ + 1)
                nc.vector.tensor_copy(eqb[:, half_], q_).then_inc(eq_ready, 1)
                dve.wait_ge(ranks_psum, part_ + 1)
                cum = PS[:, 2 * part_, 0:B // 2 * E].rearrange("p (b e) -> p b e", e=E)
                tot = PS[:, 2 * part_ + 1, 0:B // 2 * E].rearrange("p (b e) -> p b e", e=E)
                step(nc.vector.tensor_copy(scan[:, 0], tot))
                c, shift_by = 0, 1
                while shift_by < B // 2:
                    nc.vector.tensor_copy(scan[:, 1 - c, 0:shift_by], scan[:, c, 0:shift_by])
                    step(nc.vector.tensor_tensor(scan[:, 1 - c, shift_by:], scan[:, c, shift_by:],
                                                 scan[:, c, 0:B // 2 - shift_by], ALU.add))
                    c, shift_by = 1 - c, 2 * shift_by
                w = scan[:, 1 - c]
                step(nc.vector.tensor_tensor(w, scan[:, c], tot, ALU.subtract))
                step(nc.vector.tensor_tensor(w, w, cum, ALU.add))
                step(nc.vector.tensor_tensor(w, w, free_row[:, part_].unsqueeze(1).broadcast_to(shape), ALU.add))
                step(nc.vector.tensor_tensor(w, w, q_, ALU.mult))
                nc.vector.tensor_tensor(free_row[:, part_ + 1], free_row[:, part_], scan[:, c, B // 2 - 1, :], ALU.add)
                step(nc.vector.tensor_reduce(pos[:, half_], w, AX.X, ALU.add))
                step(nc.vector.tensor_copy(pos_i[:, half_], pos[:, half_]))
                dve.wait_ge(gexp_ready, part_ + 1)
                step(nc.vector.tensor_reduce(topp[:, half_], gate[:, half_], AX.X, ALU.add))
                nc.vector.reciprocal(topp[:, half_], topp[:, half_]).then_inc(pos_ready, 1)
                dve.wait_ge(pos_ready, part_ + 1)

            step(nc.vector.tensor_copy(free_row[:, 0], region0[:, 0:E]))
            route(0)
            dve.wait_ge(logits_done, NQ)
            keep_logits(NQ - 1)
            dve.wait_ge(logits_kept, NQ)
            route(1)
            step(nc.vector.tensor_tensor(counts[:], free_row[:, 2], region0[:, 0:E], ALU.subtract))
            step(nc.vector.tensor_scalar(tile_f[:], num[:], float(P), None, ALU.mult))
            step(nc.vector.tensor_tensor(cmp_k[:], counts[:].unsqueeze(2).broadcast_to([P, E, TOKENS // P]),
                                         tile_f[:, 0:TOKENS // P].unsqueeze(1).broadcast_to([P, E, TOKENS // P]), ALU.is_gt))
            step(nc.vector.tensor_reduce(tiles_of[:, 0], cmp_k[:], AX.X, ALU.add))
            step(nc.vector.tensor_scalar(gap[:], tiles_of[:, 0], -float(P), float(REGION), ALU.mult, ALU.add))
            step(nc.vector.tensor_copy(tiles_of[:, 1], tiles_of[:, 0]))
            c, shift_by = 1, 1
            while shift_by < E:
                nc.vector.tensor_copy(tiles_of[:, 3 - c, 0:shift_by], tiles_of[:, c, 0:shift_by])
                step(nc.vector.tensor_tensor(tiles_of[:, 3 - c, shift_by:E], tiles_of[:, c, shift_by:E],
                                             tiles_of[:, c, 0:E - shift_by], ALU.add))
                c, shift_by = 3 - c, 2 * shift_by
            step(nc.vector.tensor_tensor(cmp_t[:], num[:].unsqueeze(2).broadcast_to([P, NT, E]),
                                         tiles_of[:, c].unsqueeze(1).broadcast_to([P, NT, E]), ALU.is_ge))
            step(nc.vector.tensor_reduce(tile_f[:], cmp_t[:], AX.X, ALU.add))
            step(nc.vector.tensor_scalar(tile_e[:], tile_f[:], float(E - 1), None, ALU.min))
            step(nc.vector.tensor_tensor(cmp_t[:], cmp_t[:], gap[:].unsqueeze(1).broadcast_to([P, NT, E]), ALU.mult))
            step(nc.vector.tensor_reduce(tile_f[:], cmp_t[:], AX.X, ALU.add))
            step(nc.vector.scalar_tensor_tensor(tile_f[:], num[:], float(P), tile_f[:], ALU.mult, ALU.add))
            step(nc.vector.tensor_scalar(tile_row[:], tile_f[:], float(E * REGION), None, ALU.min))
            nc.vector.tensor_copy(pad_row_i[:, E:NE], region0[:, E:NE])
            step(nc.vector.tensor_copy(pad_row_i[:, 0:E], free_row[:, 2]), tables_ready)

            dve.wait_ge(ffw_in, 16 * 4)
            step(nc.vector.tensor_reduce(wabs[:], w1n[:], AX.X, ALU.add, apply_absolute_value=True))
            step(nc.vector.tensor_reduce(wabs2[:], w2n[:], AX.X, ALU.add, apply_absolute_value=True))
            step(nc.vector.tensor_scalar(wabs[:], wabs[:], 1.0 / D, 1e-5, ALU.mult, ALU.max))
            step(nc.vector.tensor_scalar(wabs2[:], wabs2[:], 1.0 / F, 1e-5, ALU.mult, ALU.max))
            for s, hh, nh in ((wabs, half, nhalf), (wabs2, half2, nhalf2)):
                step(nc.vector.tensor_scalar(hh[:], s[:], 0.5, None, ALU.mult))
                step(nc.vector.tensor_scalar(nh[:], s[:], -0.5, None, ALU.mult))
            step(nc.vector.tensor_scalar(wabs2[:], wabs2[:], tgf[:], None, ALU.mult))

            def quantise(w, s, hh, nh, neg, signal=None):
                shape = list(w.shape)
                step(nc.vector.tensor_tensor(neg, w, nh.broadcast_to(shape), ALU.is_lt))
                step(nc.vector.tensor_tensor(w, w, hh.broadcast_to(shape), ALU.is_gt))
                step(nc.vector.tensor_tensor(w, w, neg, ALU.subtract))
                if s is not None:
                    step(nc.vector.tensor_tensor(w, w, s.broadcast_to(shape), ALU.mult), signal)

            quantise(w1n[:], None, half[:].unsqueeze(3), nhalf[:].unsqueeze(3), neg1)
            quantise(w2n[:], wabs2[:].unsqueeze(2), half2[:].unsqueeze(2), nhalf2[:].unsqueeze(2),
                     neg1.rearrange("p e b d -> p e (b d)"), quantised)
            for e in range(NE):
                dve.wait_ge(wT_psum, e + 1)
                nc.vector.tensor_copy(W1T[:, e], PS[:, 2 * (e % 2), 0:F])
                nc.vector.tensor_copy(W2T[:, e], PS[:, 2 * (e % 2) + 1, 0:F]).then_inc(wT_copied, 1)

            def normalise_tile(g, k):
                n = g * SLOTS + k
                dve.wait_ge(tile_in[k], 32 * (g + 1))
                ge(dve, tileT_psum, n - 1)
                for a in range(2):
                    ins = nc.vector.tensor_scalar(xh[:, k % 2, a], tin[:, k, a, 0:D], tin[:, k, a, D:D + 1],
                                                  tin[:, k, a, D + 1:D + 2], ALU.mult, ALU.add)
                ins.then_inc(xh_ready, 1)

            def split(g, k):
                n = g * SLOTS + k
                s = k % 2
                dve.wait_ge(tileT_copied, n + 1)
                ge(dve, zr_psum, n - 1)
                for part_, (src, to) in enumerate(((hT[:, s], rest[:]), (rest[:], hpart[:, s, 2]))):
                    nc.vector.tensor_copy(hpart[:, s, part_], src).then_inc(h_part, 1)
                    dve.wait_ge(h_part, 3 * n + 2 * part_ + 1)
                    ins = nc.vector.tensor_tensor(to, src, hpart[:, s, part_], ALU.subtract)
                    if part_ == 0:
                        ins.then_inc(h_part, 1)
                        dve.wait_ge(h_part, 3 * n + 2)
                ins.then_inc(split_done, 1)

            def combine(g, k):
                n = g * SLOTS + k
                dve.wait_ge(y_psum, n + 1)
                y = PS[:, 4 + k % 2, :].rearrange("p (a w d) -> p a w d", a=2, w=2)
                nc.vector.tensor_tensor(res[:, k], tin[:, k, :, 0:D], y[:, :, 0], ALU.add).then_inc(y_sum, 1)
                dve.wait_ge(y_sum, n + 1)
                for a in range(2):
                    ins = nc.vector.scalar_tensor_tensor(res[:, k, a], y[:, a, 1], tin[:, k, a, D + 2:D + 3], res[:, k, a],
                                                         ALU.mult, ALU.add)
                ins.then_inc(res_ready, 1)

            normalise_tile(0, 0)
            normalise_tile(0, 1)
            split(0, 0)

            def group(g, first=False, last=False):
                for k in range(SLOTS):
                    if k < SLOTS - 2:
                        normalise_tile(g, k + 2)
                    elif not last:
                        normalise_tile(g + 1, k + 2 - SLOTS)
                    if k < SLOTS - 1:
                        split(g, k + 1)
                    elif not last:
                        split(g + 1, 0)
                    if k > 0:
                        combine(g, k - 1)
                    elif not first:
                        combine(g - 1, SLOTS - 1)

            group(0, first=True)
            with dve.Fori(0, NG - 2) as gi:
                group(gi + 1)
            group(NG - 1, last=True)
            combine(NG - 1, SLOTS - 1)

        @block.scalar
        def _(act):
            act.dma_start(wo_sb[:], A["Wo"][:, :]).then_inc(w_in, 16)
            act.dma_start(mask_i[:], A["mask"][0, 0]).then_inc(w_in, 16)
            for t, name in ((wq8, "Wq"), (wk8, "Wk"), (wv8, "Wv")):
                w = A[name]
                act.dma_start(t[:], bass.AP(w.tensor, w.offset, [[0, H], [HD, HD], [1, HD]])).then_inc(w_in, 16)
            act.dma_start(gx[:], A["g_x"].unsqueeze(0).broadcast_to([P, 1])).then_inc(w_in, 16)
            act.dma_start(gf[:], A["g_f"].unsqueeze(0).broadcast_to([P, 1])).then_inc(w_in, 16)
            act.dma_start(bo[:], A["bo"].unsqueeze(0).broadcast_to([P, D])).then_inc(w_in, 16)
            act.dma_start(gamma[:], A["gamma"].unsqueeze(1)).then_inc(w_in, 16)
            act.dma_start(beta[:], A["beta"].unsqueeze(1)).then_inc(w_in, 16)
            act.dma_start(rw[:], A["rw"][:, :]).then_inc(w_in, 16)
            act.dma_start(w1n[:, 0:E], A["ew1"].rearrange("e (b p) d -> p e b d", p=P)).then_inc(ffw_in, 16)
            act.dma_start(w1n[:, E], A["sw1"].rearrange("(b p) d -> p b d", p=P)).then_inc(ffw_in, 16)
            act.dma_start(w2n[:, 0:E], A["ew2"].rearrange("e d f -> d e f")).then_inc(ffw_in, 16)
            act.dma_start(w2n[:, E], A["sw2"][:, :]).then_inc(ffw_in, 16)

            act.wait_ge(w_in, 16 * N_W)
            nc.scalar.activation(tgx[:], gx[:], ACT.Tanh)
            nc.scalar.activation(tgf[:], gf[:], ACT.Tanh).then_inc(tanh_ready, 1)
            act.wait_ge(var_ready, 1)
            nc.scalar.activation(sd[:], ve[:], ACT.Sqrt).then_inc(sd_ready, 1)

            def make_xn(q):
                for j in range(QB):
                    b = q * QB + j
                    ins = nc.scalar.activation(xn[:, j, :], X[:, bass.ds(b, 1), :].squeeze(1), ACT.Identity,
                                               bias=nmr[:, bass.ds(b, 1)], scale=rstd[:, bass.ds(b, 1)])
                ins.then_inc(xn_ready, 1)

            def make_h(q):
                act.wait_ge(root_step, 11 * q + 8)
                for j in range(QB):
                    b = q * QB + j
                    if j == 0:
                        act.wait_ge(act_carried, q + 1)
                        nc.scalar.copy(act_carrier[:], gx[:]).then_inc(act_carried, 1)
                    ins = nc.scalar.activation(xn[:, j, :], X[:, bass.ds(b, 1), :].squeeze(1), ACT.Identity,
                                               bias=nmq[:, j:j + 1], scale=rsq[:, j:j + 1])
                ins.then_inc(h_ready, 1)

            def copy_h(q):
                act.wait_ge(hT_psum, q + 1)
                nc.scalar.activation(hq[:], PS[:, 6, :], ACT.Identity,
                                     bias=beta[:], scale=gamma[:]).then_inc(hT_copied, 1)

            def prep_x(q, qs):
                act.wait_ge(prep_psum, 3 * q + 1)
                nc.scalar.copy(xT[0][:, qs], PS[:, 6, :]).then_inc(xhi_done, 1)

            def prep_ctx(q):
                act.wait_ge(prep_psum, 3 * q + 2)
                nc.scalar.copy(ctxT[:], PS[:, 6, 0:QB * SK]).then_inc(prep_copied, 1)

            def prep_k(q):
                act.wait_ge(prep_psum, 3 * q + 3)
                ge(act, kbd_ready, QB * q)
                nc.scalar.copy(kp[0][:].bitcast(FP32R), PS[:, 6, 0:QB * SK]).then_inc(kp_copied, 1)

            def copy_pt(b, s, u):
                act.wait_ge(pt_psum[0], 2 * b + u + 1)
                ge(act, pv_done, b - 1)
                nc.scalar.copy(PT[:, s, 2 * u, :], PS[0:SK, 4, :]).then_inc(pt_copied[0], 1)

            def copy_mt(b, u):
                act.wait_ge(mt_psum, 2 * b + u + 1)
                ge(act, shifted, 2 * (b - 1) + u + 1)
                nc.scalar.copy(mT[:, u, :], PS[:, 6, 0:P]).then_inc(mt_copied, 1)

            def copy_spread(b):
                act.wait_ge(spread_psum, b + 1)
                ge(act, o_ready, b)
                nc.scalar.copy(rspread[:], PS[:, 6, P:2 * P]).then_inc(spread_copied, 1)

            def exps(b, s, u):
                act.wait_ge(shifted, 2 * b + u + 1)
                for v in range(2):
                    ge(act, pt_psum[v], 2 * (b - 2) + u + 1)
                ge(act, part_done, b - 1)
                nc.scalar.activation(prob[:, s, u, :, :, 0:SK],
                                     PS[:, 2 * u:2 * u + 2, 0:GK].rearrange("p g (i k) -> p g i k", k=SK), ACT.Exp,
                                     scale=float(1.0 / np.sqrt(HD))).then_inc(exp_done, 1)

            nc.scalar.copy(act_carrier[:], gx[:]).then_inc(act_carried, 1)
            act.wait_ge(stats_ready, 1)
            make_xn(0)
            prep_x(0, 0)
            prep_ctx(0)
            prep_k(0)

            def quad(q, q2, last=False):
                for j in range(QB):
                    b = q * QB + j
                    s = j % 2
                    first = isinstance(b, int) and b == 0
                    if not first:
                        copy_pt(b - 1, 1 - s, 0)
                    if j == 0 and not last:
                        make_xn(q + 1)
                    if j == 3 and not (isinstance(q, int) and q == 0):
                        make_h(q - 1)
                    copy_mt(b, 0)
                    if not isinstance(b, int) or b >= 2:
                        copy_spread(b - 2)
                    if not first:
                        copy_pt(b - 1, 1 - s, 1)
                    exps(b, s, 0)
                    copy_mt(b, 1)
                    exps(b, s, 1)
                    if not last:
                        if j == 0:
                            prep_x(q + 1, 1 - q2)
                        elif j == 1:
                            prep_ctx(q + 1)
                        elif j == 2:
                            prep_k(q + 1)
                    if j == 3 and not (isinstance(q, int) and q == 0):
                        copy_h(q - 1)

            for q in range(3):
                quad(q, q % 2)
            with act.Fori(0, (NQ - 4) // 2) as i2:
                quad(2 * i2 + 3, 1)
                quad(2 * i2 + 4, 0)
            quad(NQ - 1, 1, last=True)
            copy_pt(B - 1, 1, 0)
            copy_spread(B - 2)
            copy_pt(B - 1, 1, 1)
            copy_spread(B - 1)

            make_h(NQ - 1)
            copy_h(NQ - 1)
            def fill_pay(q, s):
                quad_ = slice(q * QB, (q + 1) * QB) if isinstance(q, int) else bass.ds(q * QB, QB)
                nc.scalar.copy(pay[:, s, :, 0:D], X[:, quad_, :])
                for col, t in ((0, rstd), (1, nmr), (2, topp)):
                    nc.scalar.copy(pay[:, s, :, D + col:D + col + 1], t[:, quad_].unsqueeze(2))
                nc.scalar.copy(pay[:, s, :, D + 3:ROW].bitcast(I32), tok_i[:, quad_].unsqueeze(2))
                nc.scalar.copy(pay_i[:, s], pos_i[:, quad_]).then_inc(pay_ready, 1)

            def exp_logits(part_):
                half_ = slice(part_ * B // 2, (part_ + 1) * B // 2)
                act.wait_ge(top_ready, part_ + 1)
                nc.scalar.activation(gate[:, half_], lg[:, half_], ACT.Exp).then_inc(gexp_ready, 1)

            exp_logits(0)
            act.wait_ge(pos_ready, 1)
            act.wait_ge(root_step, 11 * NQ)
            for s in range(PAYS):
                fill_pay(s, s)
            exp_logits(1)
            for s in range(PAYS):
                act.wait_ge(sorted_out[s], 16 * QB)
                fill_pay(PAYS + s, s)
            act.wait_ge(pos_ready, 2)
            with act.Fori(0, NQ // PAYS - 2) as i4:
                for s in range(PAYS):
                    act.wait_ge(sorted_out[s], 16 * QB * (i4 + 2))
                    act.wait_ge(act_carried, NQ + PAYS * i4 + s + 1)
                    nc.scalar.copy(act_carrier[:], gx[:]).then_inc(act_carried, 1)
                    fill_pay(PAYS * (i4 + 2) + s, s)

            def copy_tileT(g, k):
                n = g * SLOTS + k
                act.wait_ge(tileT_psum, n + 1)
                ge(act, split_done, n - 1)
                nc.scalar.activation(hT[:, k % 2], PS[:, 6, 0:2 * P], ACT.Identity,
                                     bias=beta[:], scale=gamma[:]).then_inc(tileT_copied, 1)

            def silus(g, k, experts):
                n = g * SLOTS + k
                s = k % 2
                act.wait_ge(zs_psum, n + 1)
                ge(act, y_psum, n - 1)
                for f in range(FB):
                    if f == 1:
                        act.wait_ge(zr_psum, n + 1)
                    nc.scalar.activation(h1s[:, s, f], PS[:, s, f * 2 * P:(f + 1) * 2 * P], ACT.Silu, scale=wabs[:, E, f:f + 1])
                for a in range(2):
                    for f in range(FB):
                        ins = nc.scalar.activation(h1r[:, s, a, f], PS[:, 2 + s, (2 * a + f) * P:(2 * a + f + 1) * P], ACT.Silu,
                                                   scale=wabs[:, bass.ds(experts[a], 1), f:f + 1].squeeze(1))
                ins.then_inc(silu_done, 1)

            act.wait_ge(tables_ready, 1)
            act.wait_ge(wT_copied, NE)
            copy_tileT(0, 0)

            def group(g, last=False):
                experts = nc.values_load_multi_w_load_instructions(
                    tile_e[0:1, bass.ds(2 * SLOTS * g, 2 * SLOTS)], engines=[mybir.EngineType.Activation], min_val=0, max_val=E - 1,
                    skip_runtime_bounds_check_because="tile_e is a count of 0 or more, kept to E - 1 by a minimum")[1]
                for k in range(SLOTS):
                    if k < SLOTS - 1:
                        copy_tileT(g, k + 1)
                    elif not last:
                        copy_tileT(g + 1, 0)
                    silus(g, k, experts[2 * k:2 * k + 2])

            group(0)
            with act.Fori(0, NG - 2) as gi:
                group(gi + 1)
            group(NG - 1, last=True)

        @block.tensor
        def _(pe):
            pe.wait_ge(bd_ready, 1)
            nc.tensor.transpose(PS[:, 0, 0:P], wo_sb[:], ident[:])
            nc.tensor.matmul(PS[:, 1, 0:P], wk_bd[:].rearrange("p h d -> p (h d)"),
                             wq_bd[:].rearrange("p h d -> p (h d)"), start=True, stop=True).then_inc(wo_psum, 1)
            pe.wait_ge(wo_copied, 1)
            nc.tensor.matmul(PS[:, 0, 0:P], wv_bd[:].rearrange("p h d -> p (h d)"), woT[:],
                             start=True, stop=True).then_inc(wvo_psum, 1)
            nc.tensor.transpose(PS[:, 4, 0:E], rw[:], ident[0:E, 0:E]).then_inc(rw_psum, 1)
            pe.wait_ge(rw_copied, 1)

            def prep(q, qs, part, arrived):
                if part == 0:
                    ge(pe, kp_copied, 2 * q)
                else:
                    ge(pe, prep_copied, 2 * q + part)
                if part == 0:
                    pe.wait_ge(xn_ready, q + 1)
                    for j in range(QB):
                        ins = nc.tensor.transpose(PS[:, 6, j * P:(j + 1) * P], xn[:, j, :], ident[:])
                elif part == 1:
                    pe.wait_ge(ctx_in[qs], 16 * arrived)
                    for j in range(QB):
                        ins = nc.tensor.transpose(PS[:, 6, j * SK:(j + 1) * SK],
                                                  ctxq[:, qs, j, :], ident[0:SK, 0:SK])
                else:
                    ins = nc.tensor.matmul(PS[:, 6, 0:QB * SK], MT[:], ctxT[:], start=True, stop=True)
                ins.then_inc(prep_psum, 1)

            def scores(b, j, qs, u):
                ge(pe, exp_done, 2 * (b - 1) + u + 1)
                for g in (2 * u, 2 * u + 1):
                    nc.tensor.matmul(PS[:, g, 0:GK], identb[:], maskneg[:].rearrange("p i k -> p (i k)"),
                                     start=True, stop=False)
                for n, (x, k) in enumerate(((0, 0), (1, 0), (0, 1))):
                    for g in (2 * u, 2 * u + 1):
                        r = slice(g * GR, (g + 1) * GR)
                        ins = nc.tensor.matmul(PS[:, g, 0:GK], xT[x][r, qs, j * P:(j + 1) * P],
                                               kbd[k][r, qs, j].rearrange("p i k -> p (i k)"), start=False, stop=n == 2,
                                               tile_position=(g * GR, 0))
                ins.then_inc(scores_ready, 1)

            def transpose_max(b, u, back):
                pe.wait_ge(max_ready, 2 * b + u + 1)
                ge(pe, mt_copied, 2 * b + u)
                if u == 1 and back:
                    pe.wait_ge(spread_copied, b - 1)
                nc.tensor.transpose(PS[:, 6, 0:P], nm[:, u, :], ident[:]).then_inc(mt_psum, 1)

            def shift(b, u):
                pe.wait_ge(mt_copied, 2 * b + u + 1)
                for g in (2 * u, 2 * u + 1):
                    r = slice(g * GR, (g + 1) * GR)
                    ins = nc.tensor.matmul(PS[:, g, 0:GK], mT[r, u, :], ind[r].rearrange("p i k -> p (i k)"),
                                           start=False, stop=True, tile_position=(g * GR, 0),
                                           skip_group_check=True)
                ins.then_inc(shifted, 1)

            def transpose_probs(b, s, u):
                pe.wait_ge(exp_done, 2 * b + u + 1)
                for v in range(2):
                    ge(pe, pt_copied[v], 2 * b + u)
                    for i in range(GH):
                        ins = nc.tensor.transpose(PS[0:SK, 4 + v, i * P:(i + 1) * P], prob[:, s, u, v, i, 0:SK], ident[:])
                    ins.then_inc(pt_psum[v], 1)

            def weigh(b, s, heads):
                if heads[0] == 0:
                    for v in range(2):
                        pe.wait_ge(pt_copied[v], 2 * b + 2)
                    pe.wait_ge(vm_ready, b + 1)
                    ge(pe, x1_done, b)
                for i in heads:
                    for g in range(G):
                        ins = nc.tensor.matmul(PS[g * GR:(g + 1) * GR, 7, 0:P], vm[:, s, g, i, :],
                                         PT[:, s, g, i * P:(i + 1) * P], start=i == 0, stop=i == GH - 1,
                                         tile_position=(0, g * GR))
                        if i == GH - 1 and g == G - 1:
                            ins.then_inc(pv_done, 1)

            def spread_sums(b, s, maxima):
                pe.wait_ge(rinv_done, b + 1)
                ge(pe, mt_copied, maxima)
                ge(pe, spread_copied, b)
                nc.tensor.matmul(PS[:, 6, P:2 * P], rinv[:, s].rearrange("p h d -> p (h d)"), ident[:],
                                 start=True, stop=True).then_inc(spread_psum, 1)

            def project(b, logits_of=None):
                pe.wait_ge(o_ready, b + 1)
                ins = nc.tensor.matmul(PS[:, 7, 2 * P:2 * P + D], oT[:], WVO[:], start=True, stop=True)
                if logits_of is not None:
                    ins = logits()
                ins.then_inc(proj_done, 1)

            def transpose_h(q):
                pe.wait_ge(h_ready, q + 1)
                for j in range(QB):
                    ins = nc.tensor.transpose(PS[:, 6, j * P:(j + 1) * P], xn[:, j, :], ident[:])
                ins.then_inc(hT_psum, 1)

            def logits():
                for j in range(QB):
                    ins = nc.tensor.matmul(PS[:, 7, LG + j * E:LG + (j + 1) * E],
                                           hq[:, j * P:(j + 1) * P], RWT[:], start=True, stop=True)
                return ins

            for part_ in range(3):
                prep(0, 0, part_, 1)

            def step_of(b, s, j, front, mid, back, q=None, q2=None, arrived=None, prepare=False, preps=0, keys=0,
                        h_of=None, logits_of=None, hs=0):
                if front:
                    scores(b, j, q2, 0)
                if mid:
                    transpose_probs(b - 1, 1 - s, 0)
                if front:
                    scores(b, j, q2, 1)
                    ge(pe, prep_copied, preps)
                    ge(pe, kp_copied, keys)
                    ge(pe, hT_copied, hs)
                if back:
                    spread_sums(b - 2, s, 2 * min(b, B) if isinstance(b, int) else 2 * b)
                if front:
                    transpose_max(b, 0, back)
                if mid:
                    transpose_probs(b - 1, 1 - s, 1)
                if front:
                    shift(b, 0)
                if back:
                    weigh(b - 2, s, (0, 1))
                if front:
                    transpose_max(b, 1, back)
                if back:
                    weigh(b - 2, s, (2, 3))
                if front:
                    shift(b, 1)
                if prepare and j < 3:
                    pe.wait_ge(mt_copied, 2 * b + 2)
                    prep(q + 1, 1 - q2, j, arrived)
                if h_of is not None and j == 3:
                    pe.wait_ge(mt_copied, 2 * b + 2)
                    transpose_h(h_of)
                if back:
                    project(b - 2, logits_of if j == 0 else None)

            def quad(q, q2, arrived=None, last=False):
                for j in range(QB):
                    b = q * QB + j
                    pe.wait_ge(kbd_ready, b + 1)
                    at = b if isinstance(b, int) else 2
                    done = q if last else q + 1
                    preps = 2 * (q + 1) + (0 if last else min(j, 2))
                    keys = 2 * (q + 1) + (2 if j == 3 and not last else 0)
                    nth = q if isinstance(q, int) else 2
                    step_of(b, j % 2, j, True, at >= 1, at >= 2, q, q2, arrived, not last, preps, keys,
                            h_of=q - 1 if nth >= 1 else None, logits_of=q - 2 if nth >= 2 else None,
                            hs=q - 1 if nth >= 2 else 0)

            for q in range(3):
                quad(q, q % 2, (q + 1) // 2 + 1)
            with pe.Fori(0, (NQ - 4) // 2) as i2:
                quad(2 * i2 + 3, 1, i2 + 3)
                quad(2 * i2 + 4, 0, i2 + 3)
            quad(NQ - 1, 1, last=True)
            pe.wait_ge(hT_copied, NQ - 1)
            step_of(B, 0, 0, False, True, True, logits_of=NQ - 2)
            step_of(B + 1, 1, 1, False, False, True)

            pe.wait_ge(spread_copied, B)
            transpose_h(NQ - 1)
            pe.wait_ge(hT_copied, NQ)
            pe.wait_ge(x1_done, B)
            logits().then_inc(logits_done, NQ)

            for part_ in range(2):
                half_ = eqb[:, part_ * B // 2:(part_ + 1) * B // 2].rearrange("p b e -> p (b e)")
                pe.wait_ge(eq_ready, part_ + 1)
                nc.tensor.matmul(PS[:, 2 * part_, 0:B // 2 * E], trib[:], half_, start=True, stop=True)
                nc.tensor.matmul(PS[:, 2 * part_ + 1, 0:B // 2 * E], onesb[:], half_, start=True, stop=True).then_inc(ranks_psum, 1)
            pe.wait_ge(quantised, 1)
            for e in range(NE):
                if e >= 2:
                    pe.wait_ge(wT_copied, e - 1)
                for f in range(FB):
                    nc.tensor.transpose(PS[:, 2 * (e % 2), f * P:(f + 1) * P], w1n[:, e, f, :], ident[:])
                for f in range(FB):
                    ins = nc.tensor.transpose(PS[:, 2 * (e % 2) + 1, f * P:(f + 1) * P],
                                              w2n[:, e, f * P:(f + 1) * P], ident[:])
                ins.then_inc(wT_psum, 1)

            def load_experts(first_tile, n):
                return nc.values_load_multi_w_load_instructions(
                    tile_e[0:1, bass.ds(first_tile, n)], engines=[mybir.EngineType.PE], min_val=0, max_val=E - 1,
                    skip_runtime_bounds_check_because="tile_e is a count of 0 or more, kept to E - 1 by a minimum")[1]

            def transpose_tile(g, k):
                n = g * SLOTS + k
                pe.wait_ge(xh_ready, n + 1)
                ge(pe, tileT_copied, n)
                for a in range(2):
                    ins = nc.tensor.transpose(PS[:, 6, a * P:(a + 1) * P], xh[:, k % 2, a], ident[:])
                ins.then_inc(tileT_psum, 1)

            def first_layer(g, k, experts):
                n = g * SLOTS + k
                s = k % 2
                pe.wait_ge(split_done, n + 1)
                ge(pe, silu_done, n - 1)
                for f in range(FB):
                    for h in range(3):
                        ins = nc.tensor.matmul(PS[:, s, f * 2 * P:(f + 1) * 2 * P], W1T[:, E, f, :], hpart[:, s, h],
                                               start=h == 0, stop=h == 2)
                ins.then_inc(zs_psum, 1)
                for a in range(2):
                    e = experts[a]
                    for f in range(FB):
                        for h in range(3):
                            ins = nc.tensor.matmul(PS[:, 2 + s, (2 * a + f) * P:(2 * a + f + 1) * P],
                                                   W1T[:, bass.ds(e, 1), f, :].squeeze(1), hpart[:, s, h, a * P:(a + 1) * P],
                                                   start=h == 0, stop=h == 2)
                ins.then_inc(zr_psum, 1)

            def second_layer(g, k, experts):
                n = g * SLOTS + k
                s = k % 2
                pe.wait_ge(silu_done, n + 1)
                ge(pe, res_ready, n - 1)
                for a in range(2):
                    for f in range(FB):
                        nc.tensor.matmul(PS[:, 4 + s, 2 * a * P:(2 * a + 1) * P], h1s[:, s, f, a * P:(a + 1) * P],
                                         W2T[:, E, f, :], start=f == 0, stop=f == FB - 1)
                    e = experts[a]
                    for f in range(FB):
                        ins = nc.tensor.matmul(PS[:, 4 + s, (2 * a + 1) * P:(2 * a + 2) * P], h1r[:, s, a, f],
                                               W2T[:, bass.ds(e, 1), f, :].squeeze(1), start=f == 0, stop=f == FB - 1)
                ins.then_inc(y_psum, 1)

            pe.wait_ge(tables_ready, 1)
            pe.wait_ge(wT_copied, NE)
            transpose_tile(0, 0)

            def group(g, first=False, last=False):
                experts = load_experts(0, 2 * SLOTS) if first else load_experts(2 * SLOTS * g - 4, 2 * SLOTS + 4)
                if not first:
                    before, experts = experts[2:4], experts[4:]
                for k in range(SLOTS):
                    if k < SLOTS - 1:
                        transpose_tile(g, k + 1)
                    elif not last:
                        transpose_tile(g + 1, 0)
                    first_layer(g, k, experts[2 * k:2 * k + 2])
                    if k > 0:
                        second_layer(g, k - 1, experts[2 * k - 2:2 * k])
                    elif not first:
                        second_layer(g - 1, SLOTS - 1, before)
                return experts[2 * SLOTS - 2:]

            group(0, first=True)
            with pe.Fori(0, NG - 2) as gi:
                group(gi + 1)
            second_layer(NG - 1, SLOTS - 1, group(NG - 1, last=True))


NAMES = {"x": "x", "ctx": "ctx_1024", "mask": "mask_1x1xSxS2_ik0", "g_x": "g_xattn", "g_f": "g_ffn",
         "Wq": "L0_xattn_Wq", "Wk": "L0_xattn_Wk", "Wv": "L0_xattn_Wv", "Wo": "L0_xattn_Wo", "bo": "L0_xattn_bo",
         "sw1": "L0_ffn_shared_w1", "sw2": "L0_ffn_shared_w2", "ew1": "L0_ffn_expert_w1",
         "ew2": "L0_ffn_expert_w2", "rw": "L0_ffn_router_w", "gamma": "L0_ffn_ln_gamma", "beta": "L0_ffn_ln_beta"}


def kernel(**inputs):
    import concourse.bacc as bacc
    from concourse.bass_utils import run_bass_kernel_spmd

    nc = bacc.Bacc("TRN2", target_bir_lowering=False, num_devices=1)
    arrays, args = {}, {}
    for short, name in NAMES.items():
        a = np.ascontiguousarray(inputs[name])
        arrays[f"in_{short}"] = a
        args[short] = nc.dram_tensor(f"in_{short}", a.shape, mybir.dt.from_np(a.dtype), kind="ExternalInput").ap()
    args["out"] = nc.dram_tensor("out", (B, SQ, D), FP32, kind="ExternalOutput").ap()
    args["rows"] = nc.dram_tensor("rows", (E * REGION + P, ROW), FP32, kind="Internal").ap()
    build(nc, args)
    r = run_bass_kernel_spmd(nc, [arrays], core_ids=[0])
    return r.results[0]["out"]
```
